# Optimizing a Trainium2 kernel written in Bass

```python
import numpy as np
import jax
import jax.numpy as jnp

def _softmax(x, axis=-1):
    return jax.nn.softmax(x, axis=axis)

def _gelu(x):
    return jax.nn.gelu(x, approximate=True)

def _silu(x):
    return jax.nn.silu(x)

def _sigmoid(x):
    return jax.nn.sigmoid(x)

def _layernorm(x, axis=-1, eps=1e-05):
    m = jnp.mean(x, axis=axis, keepdims=True)
    v = jnp.var(x, axis=axis, keepdims=True)
    return (x - m) / jnp.sqrt(v + eps)

def _scatter_add(tgt, idx, src, axis=0):
    return tgt.at[idx].add(src)

def _segment_sum(src, seg, n):
    return jax.ops.segment_sum(src, seg, n)
kernel_name = 'mk_adj_ffn_d1_adj_r2_f63699'

def setup_inputs(seed: int=0):
    np.random.seed(seed)
    _w = jnp.asarray

    def _rec_inputs():
        import jax
        import jax.numpy as jnp
        _gk = jax.random.key(seed)
        x = -0.0005207 + 1.001 * jax.random.normal(jax.random.fold_in(_gk, 1), (16, 512, 128), jnp.float32)
        _w = (1.0 + jnp.arange(512, dtype=jnp.float32)) ** (-0.5)
        _w = _w / _w.mean()
        _pij = jnp.clip(0.015625 * _w[:, None] * _w[None, :], 0.0, 1.0)
        _a = jax.random.uniform(jax.random.fold_in(_gk, 2), (16, 512, 512)) < _pij
        _a = jnp.logical_or(_a, jnp.eye(512, dtype=bool))
        _af = _a.astype(jnp.float32)
        _af = _af * jax.random.uniform(jax.random.fold_in(_gk, 3), (16, 512, 512), jnp.float32, 0.05, 1)
        adj = _af
        return (x, adj)
    x, adj = _rec_inputs()

    def _L0_gnn_setup():
        import math
        import jax, jax.numpy as jnp
        import numpy as np
        HIDDEN = 128
        HEADS = 8
        HEAD_DIM = HIDDEN // HEADS
        key = jax.random.key(seed)
        ks = jax.random.split(key, 8)
        b, n = (2, 2048)
        node_state = jax.random.normal(ks[0], (b, n, HIDDEN), dtype=jnp.float32)
        adjacency = jax.random.uniform(ks[1], (b, n, n), dtype=jnp.float32)
        s = 1.0 / math.sqrt(HIDDEN)
        Wq = jax.random.uniform(ks[2], (HIDDEN, HIDDEN), jnp.float32, -s, s)
        Wk = jax.random.uniform(ks[3], (HIDDEN, HIDDEN), jnp.float32, -s, s)
        Wv = jax.random.uniform(ks[4], (HIDDEN, HIDDEN), jnp.float32, -s, s)
        Wo = jax.random.uniform(ks[5], (HIDDEN, HIDDEN), jnp.float32, -s, s)
        bo = jax.random.uniform(ks[6], (HIDDEN,), jnp.float32, -s, s)
        return {'node_state': node_state, 'adjacency': adjacency, 'Wq': Wq, 'Wk': Wk, 'Wv': Wv, 'Wo': Wo, 'bo': bo}
    _L0_gnn_all = _L0_gnn_setup()
    _L0_gnn_in = {k: v for k, v in _L0_gnn_all.items() if k in ('Wq', 'Wk', 'Wv', 'Wo', 'bo')}
    del _L0_gnn_all

    def _L0_ffn_setup():
        import jax, jax.numpy as jnp
        import numpy as np
        N_EXPERTS = 8
        TOP_K = 2
        key = jax.random.key(seed)
        ks = jax.random.split(key, 5)
        B, T, C, E, H = (8, 1024, 128, 8, 341)
        scale = 1.0 / np.sqrt(C)
        return {'x': jax.random.normal(ks[0], (B, T, C), dtype=jnp.float32), 'router_w': jax.random.normal(ks[1], (E, C), dtype=jnp.float32) * scale, 'w1': jax.random.normal(ks[2], (E, H, C), dtype=jnp.float32) * scale, 'w2': jax.random.normal(ks[3], (E, C, H), dtype=jnp.float32) * (1.0 / np.sqrt(H)), 'w3': jax.random.normal(ks[4], (E, H, C), dtype=jnp.float32) * scale}
    _L0_ffn_all = _L0_ffn_setup()
    _L0_ffn_in = {k: v for k, v in _L0_ffn_all.items() if k in ('router_w', 'w1', 'w2', 'w3')}
    del _L0_ffn_all
    return {'x': x, 'adj': adj, 'L0_gnn_Wq': _L0_gnn_in['Wq'], 'L0_gnn_Wk': _L0_gnn_in['Wk'], 'L0_gnn_Wv': _L0_gnn_in['Wv'], 'L0_gnn_Wo': _L0_gnn_in['Wo'], 'L0_gnn_bo': _L0_gnn_in['bo'], 'L0_ffn_router_w': _L0_ffn_in['router_w'], 'L0_ffn_w1': _L0_ffn_in['w1'], 'L0_ffn_w2': _L0_ffn_in['w2'], 'L0_ffn_w3': _L0_ffn_in['w3']}

def reference(x, adj, L0_gnn_Wq, L0_gnn_Wk, L0_gnn_Wv, L0_gnn_Wo, L0_gnn_bo, L0_ffn_router_w, L0_ffn_w1, L0_ffn_w2, L0_ffn_w3):
    import jax
    import jax.numpy as jnp

    def _L0_gnn_ref(node_state, adjacency, Wq, Wk, Wv, Wo, bo):
        import math
        import jax, jax.numpy as jnp
        import numpy as np
        HIDDEN = 128
        HEADS = 8
        HEAD_DIM = HIDDEN // HEADS
        b, n, _ = node_state.shape

        def split_heads(x):
            return x.reshape(b, n, HEADS, HEAD_DIM).transpose(0, 2, 1, 3)
        q = split_heads(node_state @ Wq.T)
        k = split_heads(node_state @ Wk.T)
        v = split_heads(node_state @ Wv.T)
        scores = jnp.einsum('bhqd,bhkd->bhqk', q, k) / math.sqrt(HEAD_DIM)
        log_adj = jnp.log(adjacency + 1e-06)
        scores = scores + log_adj[:, None, :, :]
        attn = jax.nn.softmax(scores, axis=-1)
        out = jnp.einsum('bhqk,bhkd->bhqd', attn, v)
        out = out.transpose(0, 2, 1, 3).reshape(b, n, HIDDEN)
        return out @ Wo.T + bo

    def _L0_ffn_ref(x, router_w, w1, w2, w3):
        import jax, jax.numpy as jnp
        import numpy as np
        N_EXPERTS = 8
        TOP_K = 2
        B, T, C = x.shape
        flat = x.reshape(-1, C)
        logits = flat @ router_w.T
        probs = jax.nn.softmax(logits, axis=-1)
        topk_probs, topk_idx = jax.lax.top_k(probs, TOP_K)
        topk_probs = topk_probs / (jnp.sum(topk_probs, axis=-1, keepdims=True) + 1e-09)
        onehot = jax.nn.one_hot(topk_idx, N_EXPERTS, dtype=flat.dtype)
        gates = jnp.einsum('nk,nke->ne', topk_probs, onehot)
        h1 = jnp.einsum('nc,ehc->neh', flat, w1)
        h3 = jnp.einsum('nc,ehc->neh', flat, w3)
        h = jax.nn.silu(h1) * h3
        y = jnp.einsum('neh,ech->nec', h, w2)
        out = jnp.einsum('ne,nec->nc', gates, y)
        return out.reshape(B, T, C)
    x = x + _L0_gnn_ref(_layernorm(x, axis=-1), adj, L0_gnn_Wq, L0_gnn_Wk, L0_gnn_Wv, L0_gnn_Wo, L0_gnn_bo)
    x = x + _L0_ffn_ref(_layernorm(x, axis=-1), L0_ffn_router_w, L0_ffn_w1, L0_ffn_w2, L0_ffn_w3)
    return x

_drawn_inputs = setup_inputs


def setup_inputs(seed=0):
    import zlib

    import numpy as np

    out = dict(_drawn_inputs(seed))
    spreads = {}
    factors = {}
    for name, (base, spread) in spreads.items():
        noise = np.random.default_rng([zlib.crc32(name.encode()), seed]).standard_normal(out[name].shape)
        drawn = base * np.exp(spread * noise) if base else spread * noise
        out[name] = jnp.asarray(drawn.astype(out[name].dtype))
    for name, factor in factors.items():
        out[name] = (out[name] * factor).astype(out[name].dtype)
    return out
```

```python
import concourse.bass as bass
from concourse import mybir
from contextlib import ExitStack

F32 = mybir.dt.float32
BF16 = mybir.dt.bfloat16
ALU = mybir.AluOpType
ACT = mybir.ActivationFunctionType
AX = mybir.AxisListType

P = 128
GRAPHS, NODES, HID = 16, 512, 128
HEADS = 8
DH = HID // HEADS
TILES = NODES // P
SLOTS = 16
HALF = SLOTS // 2
GROUP = HEADS // 2
Q_PARTS = (0, 0, 0, 1, 1, 2)
K_PARTS = (0, 1, 2, 0, 1, 0)
ROWS = len(Q_PARTS) * DH
QK_DMAS = 16 * 2 * len(Q_PARTS)
ADJ_EPS = 1e-6
LN_EPS = 1e-5
EXPERTS, TOP = 8, 2
FFN = 341
FT = -(-FFN // P)
TOKENS = GRAPHS * NODES
BLOCK = 256
SUB = BLOCK // P
REGION = TOKENS + BLOCK
N_BLOCKS = TOP * TOKENS // BLOCK + EXPERTS
TRASH = EXPERTS * REGION
CONSTANTS = 9
POOL_SLOTS = (1, 4, 7, 10, 13)
N_POOL = len(POOL_SLOTS)
N_DVE = SLOTS - N_POOL


def pool_made(s):
    return sum(1 for x in POOL_SLOTS if x <= s)


def dve_made(s):
    return s + 1 - pool_made(s)


def wait_alone(eng, m, sem, value):
    if not isinstance(value, int):
        value = eng.to_reg(value)
    if not isinstance(value, int) or value > 0:
        eng.wait_ge(m.ident_ready, 1)
        eng.wait_ge(sem, value)


class Chain:

    def __init__(self, eng, sem, base):
        self.eng, self.sem, self.base, self.n = eng, sem, base, 0

    def link(self, ins, m=None):
        self.n += 1
        ins.then_inc(self.sem, 1)
        if m is None:
            self.eng.wait_ge(self.sem, self.base + self.n)
        else:
            wait_alone(self.eng, m, self.sem, self.base + self.n)


class Memory:
    pass


def place(nc, ctx):
    m = Memory()

    def sb(name, shape, dt=F32):
        return ctx.enter_context(nc.sbuf_tensor(name, shape, dt))

    def sem(name):
        return ctx.enter_context(nc.semaphore(name))

    m.x = sb("x_all", [P, GRAPHS * TILES, HID])
    m.ident = sb("ident", [P, P])
    m.wq, m.wk, m.wv, m.wo = (sb(n, [P, HID]) for n in ("wqT", "wkT", "wvT", "woT"))
    m.bo = sb("bo_rows", [P, HID])
    m.router = sb("routerT", [P, EXPERTS])
    m.before = sb("before_me", [P, P])
    m.ones = sb("all_ones", [P, P])
    m.small = sb("small_constants", [P, 2 * EXPERTS])
    m.blocks = sb("block_numbers", [P, N_BLOCKS])
    m.gates = sb("gates", [P, GRAPHS * TILES, TOP])
    m.pos = sb("row_of_choice", [P, GRAPHS * TILES, TOP])
    m.chosen = sb("expert_of_choice", [P, GRAPHS * TILES, TOP])
    m.counts = sb("seen_before", [P, TILES + 1, EXPERTS])
    m.psum = ctx.enter_context(nc.psum_tensor("psum", [P, 8, 512], F32))
    m.sb, m.sem = sb, sem
    m.const_in = sem("const_in")
    m.ident_ready = sem("ident_ready")
    return m


def stage_projections(nc, m, x_d, w_d, qk_d, v_d):
    with ExitStack() as ctx:
        def sb(name, shape, dt=F32):
            return ctx.enter_context(nc.sbuf_tensor(name, shape, dt))

        def sem(name):
            return ctx.enter_context(nc.semaphore(name))

        stats = sb("ln_stats", [P, 2, TILES, 6])
        mv = sb("ln_mean_var", [P, 2, TILES, 2])
        var_eps = sb("ln_var_eps", [P, 2, TILES])
        minus_half = sb("minus_half", [P, TILES])
        rstd = sb("ln_rstd", [P, 2, TILES])
        xn = sb("xn", [P, 2, TILES, HID])
        xnT = sb("xnT", [P, 2, NODES])
        parts = sb("qk_parts", [P, 2, 6, NODES], BF16)
        rest = sb("qk_rest", [P, 2, 2, NODES])
        vpad = sb("v_padded", [P, 2, TILES, HEADS, 32])

        x_in = [sem("x_in0"), sem("x_in1")]
        half_ready, var_ready, rstd_ready = sem("half_ready"), sem("var_ready"), sem("rstd_ready")
        xn_ready, xnT_psum, xnT_ready = sem("xn_ready"), sem("xnT_psum"), sem("xnT_ready")
        q_psum, k_psum, v_psum = sem("q_psum"), sem("k_psum"), sem("v_psum")
        high_ready, rest_ready, mid_ready = sem("high_ready"), sem("rest_ready"), sem("mid_ready")
        low_ready, v_ready, vpad_init = sem("low_ready"), sem("v_ready"), sem("vpad_init")
        biased = sem("residual_biased")
        stored = [sem("stacks_stored0"), sem("stacks_stored1")]
        dve_chain = sem("s1_dve_chain")
        DVE_LINKS = 2

        def rounds(eng, body):
            with eng.Fori(0, GRAPHS // 2) as n:
                for u in (0, 1):
                    body(n, u)

        with nc.Block() as block:
            @block.sync
            def _(sp):
                for t, d in ((m.wq, w_d[0]), (m.wk, w_d[1]), (m.wv, w_d[2]), (m.wo, w_d[3])):
                    sp.dma_start(t[:, :], d).then_inc(m.const_in, 16)
                for t, d in ((m.bo, w_d[4]), (m.router, w_d[5]), (m.before, w_d[6]),
                             (m.small, w_d[7]), (m.blocks, w_d[8])):
                    sp.dma_start(t[:, :], d).then_inc(m.const_in, 16)

                def loads(n, u):
                    b = 2 * n + u
                    sp.wait_ge(xn_ready, b + 1)
                    sp.dma_start(m.x[:, bass.ds(b * TILES, TILES), :],
                                 x_d[b, :, :].rearrange("(t p) c -> p t c", p=P)).then_inc(x_in[u], 16)
                rounds(sp, loads)
                for u in (0, 1):
                    sp.wait_ge(stored[u], 32 * (GRAPHS // 2) + 32)

            @block.gpsimd
            def _(pool):
                pool.memset(m.ident[:, :], 0.0).then_inc(m.ident_ready, 1)
                pool.wait_ge(m.ident_ready, 1)
                pool.affine_select(out=m.ident[:, :], in_=m.ident[:, :], compare_op=ALU.not_equal,
                                   fill=1.0, base=0, pattern=[[-1, P]], channel_multiplier=1
                                   ).then_inc(m.ident_ready, 1)
                pool.memset(m.ones[:, :], 1.0).then_inc(half_ready, 1)
                pool.memset(m.counts[:, :, :], 0.0).then_inc(half_ready, 1)
                pool.memset(minus_half[:, :], -0.5).then_inc(half_ready, 1)
                pool.wait_ge(half_ready, 3)
                pool.memset(vpad[:, :, :, :, :], 0.0).then_inc(vpad_init, 1)
                pool.wait_ge(vpad_init, 1)
                pool.memset(vpad[:, :, :, :, DH:DH + 1], 1.0).then_inc(vpad_init, 1)
                pool.wait_ge(m.const_in, CONSTANTS * 16)

                def invert(n, u):
                    b = 2 * n + u
                    pool.wait_ge(var_ready, b + 1)
                    pool.tensor_tensor(rstd[:, u, :], var_eps[:, u, :], minus_half[:, :],
                                       ALU.pow).then_inc(rstd_ready, 1)

                def low(n, u):
                    b = 2 * n + u
                    for j in range(2):
                        pool.wait_ge(mid_ready, 2 * b + j + 1)
                        pool.tensor_tensor(parts[:, u, 3 * j + 2, :], rest[:, u, j, :],
                                           parts[:, u, 3 * j + 1, :], ALU.subtract).then_inc(low_ready, 1)
                    xb = m.x[:, bass.ds(b * TILES, TILES), :]
                    pool.tensor_tensor(xb, xb, m.bo[:, :].unsqueeze(1).to_broadcast([P, TILES, HID]),
                                       ALU.add).then_inc(biased, 1)

                invert(0, 0)
                with pool.Fori(0, GRAPHS // 2 - 1) as n:
                    invert(n, 1)
                    low(n, 0)
                    invert(n + 1, 0)
                    low(n, 1)
                invert(GRAPHS // 2 - 1, 1)
                low(GRAPHS // 2 - 1, 0)
                low(GRAPHS // 2 - 1, 1)
                pool.wait_ge(biased, GRAPHS)

            @block.vector
            def _(dve):
                dve.sem_inc(xn_ready, 2)

                def norm(n, u):
                    b = 2 * n + u
                    c = Chain(dve, dve_chain, DVE_LINKS * b)
                    wait_alone(dve, m, x_in[u], 16 * (n + 1))
                    for t in range(TILES):
                        last = dve.bn_stats(stats[:, u, t, :], m.x[:, b * TILES + t, :])
                    c.link(last, m)
                    for t in range(TILES):
                        last = dve.bn_aggr(mv[:, u, t, :], stats[:, u, t, :])
                    c.link(last)
                    dve.tensor_scalar_add(var_eps[:, u, :], mv[:, u, :, 1], LN_EPS).then_inc(var_ready, 1)
                    dve.wait_ge(rstd_ready, b + 1)
                    dve.wait_ge(xnT_psum, b + 1)
                    for t in range(TILES):
                        last = dve.tensor_scalar(xn[:, u, t, :], m.x[:, b * TILES + t, :],
                                                 mv[:, u, t, 0:1], rstd[:, u, t:t + 1],
                                                 ALU.subtract, ALU.mult)
                    last.then_inc(xn_ready, 1)

                def split(n, u):
                    b = 2 * n + u
                    for j in range(2):
                        dve.wait_ge(high_ready, 2 * b + j + 1)
                        dve.wait_ge(low_ready, 2 * b + j + 1)
                        dve.tensor_tensor(rest[:, u, j, :], m.psum[:, 2 + 2 * j + u, :],
                                          parts[:, u, 3 * j, :], ALU.subtract).then_inc(rest_ready, 1)
                        dve.wait_ge(rest_ready, 2 * b + j + 1 + 4)
                        dve.tensor_copy(parts[:, u, 3 * j + 1, :], rest[:, u, j, :]).then_inc(mid_ready, 1)

                dve.sem_inc(low_ready, 4)
                dve.sem_inc(rest_ready, 4)
                dve.sem_inc(xnT_psum, 2)
                norm(0, 0)
                with dve.Fori(0, GRAPHS // 2 - 1) as n:
                    norm(n, 1)
                    split(n, 0)
                    norm(n + 1, 0)
                    split(n, 1)
                norm(GRAPHS // 2 - 1, 1)
                split(GRAPHS // 2 - 1, 0)
                split(GRAPHS // 2 - 1, 1)

            @block.tensor
            def _(pe):
                pe.wait_ge(m.ident_ready, 2)
                pe.wait_ge(m.const_in, CONSTANTS * 16)

                def body(n, u):
                    b = 2 * n + u
                    pe.wait_ge(xn_ready, b + 1 + 2)
                    pe.wait_ge(xnT_ready, b + 1)
                    for t in range(TILES):
                        last = pe.transpose(m.psum[:, u, t * P:(t + 1) * P], xn[:, u, t, :], m.ident[:, :])
                    last.then_inc(xnT_psum, 1)
                    pe.wait_ge(xnT_ready, b + 1 + 2)
                    pe.wait_ge(rest_ready, 2 * b + 1)
                    pe.matmul(m.psum[:, 2 + u, :], m.wq[:, :], xnT[:, u, :],
                              start=True, stop=True).then_inc(q_psum, 1)
                    pe.wait_ge(rest_ready, 2 * b + 2)
                    pe.matmul(m.psum[:, 4 + u, :], m.wk[:, :], xnT[:, u, :],
                              start=True, stop=True).then_inc(k_psum, 1)
                    pe.wait_ge(v_ready, b + 1)
                    for t in range(TILES):
                        last = pe.matmul(m.psum[:, 6 + u, t * P:(t + 1) * P],
                                         xnT[:, u, t * P:(t + 1) * P], m.wv[:, :], start=True, stop=True)
                    last.then_inc(v_psum, 1)
                rounds(pe, body)

            @block.scalar
            def _(act):
                act.sem_inc(xnT_ready, 2)
                act.sem_inc(v_ready, 2)
                act.sem_inc(stored[0], 32)
                act.sem_inc(stored[1], 32)
                act.wait_ge(vpad_init, 2)

                def body(n, u):
                    b = 2 * n + u
                    act.wait_ge(xnT_psum, b + 1 + 2)
                    act.wait_ge(v_psum, b + 1)
                    act.copy(xnT[:, u, :], m.psum[:, u, :]).then_inc(xnT_ready, 1)
                    act.wait_ge(stored[u], 32 * n + 32)
                    act.wait_ge(q_psum, b + 1)
                    act.copy(parts[:, u, 0, :], m.psum[:, 2 + u, :]).then_inc(high_ready, 1)
                    act.wait_ge(k_psum, b + 1)
                    act.copy(parts[:, u, 3, :], m.psum[:, 4 + u, :]).then_inc(high_ready, 1)
                    act.wait_ge(v_psum, b + 1 + 2)
                    act.copy(vpad[:, u, :, :, 0:DH],
                             m.psum[:, 6 + u, :].rearrange("p (t h d) -> p t h d", t=TILES, h=HEADS)
                             ).then_inc(v_ready, 1)
                    act.wait_ge(v_ready, b + 1 + 2)
                    act.dma_start(v_d[b, :, :], vpad[:, u, :, :, :].rearrange("p t h c -> p (t h c)")
                                  ).then_inc(stored[u], 16)
                    act.wait_ge(low_ready, 2 * b + 2 + 4)
                    act.dma_start(qk_d[b, :, :, :].rearrange("s p c -> p s c"),
                                  parts[:, u, :, :]).then_inc(stored[u], 16)
                act.sem_inc(v_psum, 2)
                rounds(act, body)


def stage_attention(nc, m, adj_d, qk_d, v_d, rows_d):
    with ExitStack() as ctx:
        def sb(name, shape, dt=F32):
            return ctx.enter_context(nc.sbuf_tensor(name, shape, dt))

        def sem(name):
            return ctx.enter_context(nc.semaphore(name))

        qs = sb("q_stack", [P, 4, GROUP, NODES], BF16)
        ks = sb("k_stack", [P, 4, GROUP, NODES], BF16)
        vp = sb("v_pad", [P, 2, TILES, HEADS, 32])
        adj = sb("adj_T", [P, 2, TILES, NODES])
        ex = sb("exp_for_pool", [P, 2, 2, NODES])
        pr = sb("products", [P, 4, 2, NODES])
        mx = sb("minus_max", [P, 4, 16])
        mx_parts = sb("minus_max_parts", [16, 2, 3, P], BF16)
        mx_rest = sb("minus_max_rest", [16, 2, P])
        osb = sb("values_T", [P, NODES])
        rec = sb("row_sum_inverse", [P, TILES, GROUP])
        an = sb("attended", [P, TILES, HID])
        anT = sb("attended_T", [P, NODES])

        stats = sb("ln2_stats", [P, TILES, 6])
        mv = sb("ln2_mean_var", [P, TILES, 2])
        var_eps = sb("ln2_var_eps", [P, TILES])
        minus_half = sb("ln2_minus_half", [P, TILES])
        rstd = sb("ln2_rstd", [P, TILES])
        xn = sb("xn2", [P, 2, TILES, HID])
        xnT = sb("xn2_T", [P, NODES])
        lmax = sb("minus_max_logit", [P, TILES])
        prob = sb("router_probs", [P, TILES, EXPERTS])
        psum_inv = sb("prob_sum", [P, 2, TILES])
        top = sb("top_probs", [P, TILES, 8])
        topi = sb("top_experts", [P, TILES, 8], mybir.dt.uint32)
        topf = sb("chosen_experts", [P, TILES, TOP])
        tsum = sb("top_sum", [P, 2, TILES])
        hot = sb("choice_one_hot", [P, TILES, TOP, EXPERTS])
        given = sb("given_to", [P, TILES, EXPERTS])
        rank = sb("rank_rows", [P, TILES, EXPERTS])
        picked = sb("rank_picked", [P, TILES, TOP, EXPERTS])
        posf = sb("row_float", [P, TILES, TOP])
        pos2 = sb("row_index", [P, 2, TILES, TOP], mybir.dt.uint32)

        var_ready, rstd_ready, xn_ready = sem("ln2_var_ready"), sem("ln2_rstd_ready"), sem("xn2_ready")
        xnT_psum, xnT_ready = sem("xn2_turned"), sem("xn2_T_ready")
        lg_psum, lg_read, prob_exp = sem("logits_ready"), sem("logits_read"), sem("probs_exp")
        given_ready, rank_psum, rank_read = sem("given_ready"), sem("ranks_ready"), sem("ranks_read")
        pos_ready, scattered = sem("rows_ready"), [sem("scattered0"), sem("scattered1")]
        chain_sem = sem("route_chain")
        ones_ready = sem("ones_ready")
        qk_loaded = [sem(f"qk_loaded{g}") for g in range(4)]
        shift_loaded = [sem(f"shift_loaded{g}") for g in range(4)]
        adj_loaded = [sem(f"adj_loaded{u}") for u in (0, 1)]
        v_loaded = [sem(f"v_loaded{u}") for u in (0, 1)]
        adj_ready = sem("adj_eps_added")
        st_ready, st_free = sem("scores_ready"), [sem("scores_free0"), sem("scores_free1")]
        sm_ready, max_done = sem("scores_for_max"), sem("max_done")
        exp_dve, exp_pool = sem("exp_for_dve"), sem("exp_for_pool_s")
        made_dve, made_pool = sem("products_of_dve"), sem("products_of_pool")
        pv_done, osb_ready = sem("values_summed"), sem("values_copied")
        mt_psum, mt_high, mt_rest, mt_mid, mt_low = (sem(n) for n in (
            "max_turned", "max_high", "max_rest", "max_mid", "max_low"))
        ot_psum, rec_ready, an_ready = sem("values_turned"), sem("sums_inverted"), sem("attended_ready")
        at_psum, at_ready = sem("attended_turned"), sem("attended_T_ready")
        wo_psum, x1_ready = sem("output_ready"), sem("x1_ready")

        ST = [m.psum[:, 0:2, :], m.psum[:, 2:4, :]]
        SM = m.psum[:, 4:6, :]
        OT = m.psum[:, 6, :]
        MISC = m.psum[:, 7, :]

        def every_graph(body):
            def walk(eng):
                body(-1, -1, 1, False, True, False, False)
                body(0, 0, 0, True, True, False, False)
                body(1, 0, 1, True, True, True, False)
                with eng.Fori(0, GRAPHS // 2 - 2) as i:
                    body(2 * i + 2, i + 1, 0, True, True, True, True)
                    body(2 * i + 3, i + 1, 1, True, True, True, True)
                body(GRAPHS - 2, GRAPHS // 2 - 1, 0, True, True, True, True)
                body(GRAPHS - 1, GRAPHS // 2 - 1, 1, True, False, True, True)
                body(GRAPHS, GRAPHS // 2, 0, False, False, True, True)
                body(GRAPHS + 1, GRAPHS // 2, 1, False, False, False, True)
            return walk

        def wait_pos(eng, s, value):
            if not isinstance(value, int) or value > 0:
                eng.wait_ge(s, value)

        with nc.Block() as block:
            @block.sync
            def _(sp):
                def load_group(b, n, u, g):
                    buf = 2 * u + g
                    wait_pos(sp, qk_loaded[buf], QK_DMAS * n)
                    cols = slice(g * GROUP * NODES, (g + 1) * GROUP * NODES)
                    for stack, first, order in ((qs, 0, Q_PARTS), (ks, 3, K_PARTS)):
                        for j, part in enumerate(order):
                            src = qk_d[b, first + part, :, :].rearrange("(d h) c -> d (h c)", d=DH)
                            sp.dma_start(stack[DH * j:DH * (j + 1), buf, :, :].rearrange("d h c -> d (h c)"),
                                         src[:, cols]).then_inc(qk_loaded[buf], 16)

                def load_adj(b, n, u):
                    sp.dma_start(adj[:, u, :, :], adj_d[b, :, :].rearrange("(t p) q -> p t q", p=P)
                                 ).then_inc(adj_loaded[u], 16)

                def load_v(b, n, u):
                    sp.dma_start(vp[:, u, :, :, :].rearrange("p t h c -> p (t h c)"), v_d[b, :, :]
                                 ).then_inc(v_loaded[u], 16)

                def load_shift(b, n, u, g):
                    y = g
                    sp.wait_ge(mt_low, 2 * b + g + 1)
                    for part in range(3):
                        sp.dma_start(qs[ROWS + part:ROWS + part + 1, 2 * u + g, :, :].rearrange(
                                         "o h (t p) -> o (h t) p", p=P),
                                     mx_parts[:, y, part, :]
                                     ).then_inc(shift_loaded[2 * u + g], 16)

                def body(b, n, u, scores, maxima, tail, ranks):
                    v, nv = 1 - u, n + u
                    if maxima:
                        wait_pos(sp, st_ready, SLOTS * b)
                        load_group(b + 1, nv, v, 1)
                        if scores:
                            wait_alone(sp, m, made_dve, N_DVE * b)
                            wait_pos(sp, made_pool, N_POOL * b)
                            load_adj(b + 1, nv, v)
                    if scores:
                        load_shift(b, n, u, 1)
                    if maxima:
                        if scores:
                            wait_pos(sp, pv_done, HALF * b)
                            load_v(b + 1, nv, v)
                        if not isinstance(b, int) or b < GRAPHS - 2:
                            if scores:
                                sp.wait_ge(st_ready, SLOTS * b + HALF)
                            load_group_next(b, n, u)
                        load_shift(b + 1, nv, v, 0)

                def load_group_next(b, n, u):
                    load_group(b + 2, n + 1, u, 0)

                load_group(0, 0, 0, 0)
                load_adj(0, 0, 0)
                load_v(0, 0, 0)
                every_graph(body)(sp)

            @block.gpsimd
            def _(pool):
                pool.memset(ks[ROWS:ROWS + 3, :, :, :], 1.0).then_inc(ones_ready, 1)
                pool.wait_ge(ones_ready, 1)

                pool.memset(minus_half[:, :], -0.5).then_inc(ones_ready, 1)
                pool.wait_ge(ones_ready, 2)

                def product(b, n, u, s):
                    k, kt = POOL_SLOTS.index(s), s % HALF // 2
                    pool.wait_ge(exp_pool, N_POOL * b + k + 1)
                    wait_pos(pool, pv_done, HALF * b + (s - 4) // 2 + 1)
                    e = (N_POOL * u + k) % 2
                    pool.tensor_tensor(pr[:, s % 4, :, :], ex[:, e, :, :],
                                       adj[:, u, kt, :].unsqueeze(1).to_broadcast([P, 2, NODES]),
                                       ALU.mult).then_inc(made_pool, 1)

                def scatter(c, cu, t):
                    if t == 0:
                        wait_alone(pool, m, pos_ready, c + 1)
                    for k in range(TOP):
                        pool.indirect_dma_start(
                            rows_d[:, :], bass.IndirectOffsetOnAxis(ap=pos2[:, cu, t, k:k + 1], axis=0),
                            xn[:, cu, t, :], None).then_inc(scattered[cu], 16)

                def body(b, n, u, scores, maxima, tail, ranks):
                    if scores:
                        wait_alone(pool, m, adj_loaded[u], 16 * n + 16)
                        pool.tensor_scalar(adj[:, u, :, :], adj[:, u, :, :], ADJ_EPS, 1.0,
                                           ALU.add, ALU.mult).then_inc(adj_ready, 1)
                        pool.wait_ge(adj_ready, b + 1)
                    for s in range(SLOTS):
                        if scores and s in POOL_SLOTS:
                            product(b, n, u, s)
                        if ranks and s in (2, 5, 8, 11):
                            scatter(b - 2, u, (s - 2) // 3)
                        if s == 9 and tail:
                            pool.wait_ge(var_ready, b)
                            pool.tensor_tensor(rstd[:, :], var_eps[:, :], minus_half[:, :],
                                               ALU.pow).then_inc(rstd_ready, 1)
                every_graph(body)(pool)
                for u in (0, 1):
                    pool.wait_ge(scattered[u], 16 * TILES * TOP * GRAPHS // 2)

            @block.scalar
            def _(act):
                def values_copy(b, g):
                    act.wait_ge(pv_done, HALF * b + 4 * g + 4)
                    wait_pos(act, ot_psum, 2 * b + g)
                    act.copy(osb[:, :], OT).then_inc(osb_ready, 1)

                def max_high(b, g):
                    y = g
                    act.wait_ge(mt_psum, 2 * b + g + 1)
                    act.copy(mx_parts[:, y, 0, :], MISC[0:16, 0:P]).then_inc(mt_high, 1)

                def body(b, n, u, scores, maxima, tail, ranks):
                    for s in range(SLOTS):
                        kt, pair, g = s % HALF // 2, s % 2, s // HALF
                        if scores:
                            act.wait_ge(st_ready, SLOTS * b + s + 1)
                            if s in POOL_SLOTS:
                                k = POOL_SLOTS.index(s)
                                e = (N_POOL * u + k) % 2
                                wait_pos(act, made_pool, N_POOL * b + k - 1)
                                act.activation(ex[:, e, :, :], ST[s % 2], ACT.Exp, scale=DH ** -0.5
                                               ).then_inc(exp_pool, 1)
                                act.wait_ge(exp_pool, N_POOL * b + k + 1)
                                act.sem_inc(st_free[s % 2], 1)
                            else:
                                act.activation(ST[s % 2], ST[s % 2], ACT.Exp, scale=DH ** -0.5
                                               ).then_inc(exp_dve, 1)
                        if s == 0 and scores:
                            max_high(b, 1)
                        if s == 1 and tail:
                            values_copy(b - 1, 1)
                        if s == 5 and tail:
                            act.wait_ge(at_psum, b)
                            wait_pos(act, wo_psum, b - 1)
                            act.copy(anT[:, :], MISC).then_inc(at_ready, 1)
                        if s == 8 and maxima:
                            max_high(b + 1, 0)
                        if s == 9 and scores:
                            values_copy(b, 0)
                        if s == 12 and tail:
                            act.wait_ge(xnT_psum, b)
                            act.copy(xnT[:, :], MISC).then_inc(xnT_ready, 1)
                        if s == 14 and tail:
                            act.wait_ge(lg_read, b)
                            act.activation(prob[:, :, :], prob[:, :, :], ACT.Exp).then_inc(prob_exp, 1)
                every_graph(body)(act)

            @block.vector
            def _(dve):
                dve.sem_inc(st_free[0], 1)
                dve.sem_inc(st_free[1], 1)

                def max_low(b, g):
                    i, y = 2 * b + g, g
                    dve.wait_ge(mt_high, i + 1)
                    dve.tensor_tensor(mx_rest[:, y, :], MISC[0:16, 0:P], mx_parts[:, y, 0, :],
                                      ALU.subtract).then_inc(mt_rest, 1)
                    dve.wait_ge(mt_rest, i + 1)
                    dve.tensor_copy(mx_parts[:, y, 1, :], mx_rest[:, y, :]).then_inc(mt_mid, 1)
                    dve.wait_ge(mt_mid, i + 1)
                    dve.tensor_tensor(mx_parts[:, y, 2, :], mx_rest[:, y, :], mx_parts[:, y, 1, :],
                                      ALU.subtract).then_inc(mt_low, 1)

                def normalise(b, g):
                    i = 2 * b + g
                    t = MISC.rearrange("p (t j c) -> p t j c", t=TILES, c=32)
                    dve.wait_ge(ot_psum, i + 1)
                    dve.reciprocal(rec[:, :, :], t[:, :, :, DH]).then_inc(rec_ready, 1)
                    dve.wait_ge(rec_ready, i + 1)
                    if g == 0:
                        wait_pos(dve, at_psum, b)
                    out = an[:, :, g * 64:g * 64 + 64].rearrange("p t (j d) -> p t j d", d=DH)
                    dve.tensor_tensor(out, t[:, :, :, 0:DH],
                                      rec[:, :, :].unsqueeze(3).to_broadcast([P, TILES, GROUP, DH]),
                                      ALU.mult).then_inc(an_ready, 1)

                LINKS, AT_ROUTE, AT_PICK = 20, 2, 18

                def norm_stats(c):
                    ch = Chain(dve, chain_sem, LINKS * c)
                    for t in range(TILES):
                        last = dve.bn_stats(stats[:, t, :], m.x[:, c * TILES + t, :])
                    ch.link(last, m)
                    for t in range(TILES):
                        last = dve.bn_aggr(mv[:, t, :], stats[:, t, :])
                    ch.link(last)
                    dve.tensor_scalar_add(var_eps[:, :], mv[:, :, 1], LN_EPS).then_inc(var_ready, 1)

                def norm(c, cn, cu):
                    dve.wait_ge(rstd_ready, c + 1)
                    wait_pos(dve, scattered[cu], 16 * TILES * TOP * cn)
                    for t in range(TILES):
                        last = dve.tensor_scalar(xn[:, cu, t, :], m.x[:, c * TILES + t, :],
                                                 mv[:, t, 0:1], rstd[:, t:t + 1],
                                                 ALU.subtract, ALU.mult)
                    last.then_inc(xn_ready, 1)

                def logits_shift(c):
                    ch = Chain(dve, chain_sem, LINKS * c + AT_ROUTE)
                    lg = MISC[:, 0:TILES * EXPERTS].rearrange("p (t e) -> p t e", e=EXPERTS)
                    dve.wait_ge(lg_psum, c + 1)
                    ch.link(dve.tensor_reduce(lmax[:, :], lg, AX.X, ALU.max, negate=True))
                    dve.tensor_tensor(prob[:, :, :], lg,
                                      lmax[:, :].unsqueeze(2).to_broadcast([P, TILES, EXPERTS]),
                                      ALU.add).then_inc(lg_read, 1)

                def choose(c):
                    ch = Chain(dve, chain_sem, LINKS * c + AT_ROUTE + 1)
                    dve.wait_ge(prob_exp, c + 1)
                    ch.link(dve.tensor_reduce(psum_inv[:, 0, :], prob[:, :, :], AX.X, ALU.add))
                    ch.link(dve.reciprocal(psum_inv[:, 1, :], psum_inv[:, 0, :]))
                    ch.link(dve.tensor_tensor(
                        prob[:, :, :], prob[:, :, :],
                        psum_inv[:, 1, :].unsqueeze(2).to_broadcast([P, TILES, EXPERTS]), ALU.mult), m)
                    for t in range(TILES):
                        last = dve.max(top[:, t, :], prob[:, t, :])
                    ch.link(last, m)
                    for t in range(TILES):
                        last = dve.max_index(topi[:, t, :], top[:, t, :], prob[:, t, :])
                    ch.link(last)
                    dve.tensor_copy(topf[:, :, :], topi[:, :, 0:TOP])
                    ch.link(dve.tensor_tensor(tsum[:, 0, :], top[:, :, 0], top[:, :, 1], ALU.add))
                    ch.link(dve.tensor_scalar_add(tsum[:, 0, :], tsum[:, 0, :], 1e-9))
                    ch.link(dve.reciprocal(tsum[:, 1, :], tsum[:, 0, :]))
                    dve.tensor_tensor(m.gates[:, bass.ds(c * TILES, TILES), :], top[:, :, 0:TOP],
                                      tsum[:, 1, :].unsqueeze(2).to_broadcast([P, TILES, TOP]), ALU.mult)
                    ch.link(dve.tensor_tensor(
                        hot[:, :, :, :].rearrange("p t k e -> p (t k) e"),
                        m.small[:, 0:EXPERTS].unsqueeze(1).to_broadcast([P, TILES * TOP, EXPERTS]),
                        topf[:, :, :].rearrange("p t k -> p (t k)").unsqueeze(2).to_broadcast(
                            [P, TILES * TOP, EXPERTS]), ALU.is_equal))
                    ch.link(dve.tensor_copy(m.counts[:, 0, :], m.counts[:, TILES, :]))
                    ch.link(dve.tensor_tensor(given[:, :, :], hot[:, :, 0, :], hot[:, :, 1, :], ALU.add))
                    for t in range(TILES):
                        last = dve.tensor_tensor(m.counts[:, t + 1, :], m.counts[:, t, :], given[:, t, :],
                                                 ALU.add)
                        ch.link(last)
                    assert AT_ROUTE + 1 + ch.n == AT_PICK
                    dve.sem_inc(given_ready, 1)

                def pick_rows(c, cu):
                    ch = Chain(dve, chain_sem, LINKS * c + AT_PICK)
                    dve.wait_ge(rank_psum, c + 1)
                    rk = MISC[:, 0:TILES * EXPERTS].rearrange("p (t e) -> p t e", e=EXPERTS)
                    dve.tensor_tensor(rank[:, :, :], rk, m.small[:, EXPERTS:2 * EXPERTS].unsqueeze(1)
                                      .to_broadcast([P, TILES, EXPERTS]), ALU.add).then_inc(rank_read, 1)
                    dve.wait_ge(rank_read, c + 1)
                    ch.link(dve.tensor_tensor(
                        picked[:, :, :, :], hot[:, :, :, :],
                        rank[:, :, :].unsqueeze(2).to_broadcast([P, TILES, TOP, EXPERTS]), ALU.mult))
                    ch.link(dve.tensor_reduce(posf[:, :, :], picked[:, :, :, :], AX.X, ALU.add))
                    assert AT_PICK + ch.n == LINKS
                    dve.tensor_copy(m.pos[:, bass.ds(c * TILES, TILES), :], posf[:, :, :])
                    dve.tensor_copy(m.chosen[:, bass.ds(c * TILES, TILES), :], topf[:, :, :])
                    dve.tensor_copy(pos2[:, cu, :, :], posf[:, :, :]).then_inc(pos_ready, 1)

                def body(b, n, u, scores, maxima, tail, ranks):
                    for s in range(SLOTS):
                        kt, pair, g = s % HALF // 2, s % 2, s // HALF
                        if maxima:
                            i = SLOTS * (b + 1) + s
                            col = (s % HALF // 2) * TILES + 2 * (s % 2)
                            dve.wait_ge(sm_ready, i + 1)
                            dve.tensor_reduce(mx[:, 2 * (1 - u) + g, col:col + 2], SM, AX.X, ALU.max,
                                              negate=True).then_inc(max_done, 1)
                        if scores and s not in POOL_SLOTS:
                            k = dve_made(s) - 1
                            if k == 0:
                                dve.wait_ge(adj_ready, b + 1)
                            dve.wait_ge(exp_dve, N_DVE * b + k + 1)
                            wait_pos(dve, pv_done, HALF * b + (s - 4) // 2 + 1)
                            dve.tensor_tensor(pr[:, s % 4, :, :], ST[s % 2],
                                              adj[:, u, kt, :].unsqueeze(1).to_broadcast([P, 2, NODES]),
                                              ALU.mult).then_inc(made_dve, 1)
                            dve.wait_ge(made_dve, N_DVE * b + k + 1)
                            dve.sem_inc(st_free[s % 2], 1)
                        if s == 0 and scores:
                            max_low(b, 1)
                        if s == 3 and tail:
                            normalise(b - 1, 1)
                        if s == 7 and tail:
                            xb = m.x[:, bass.ds((b - 1) * TILES, TILES), :]
                            dve.wait_ge(wo_psum, b)
                            dve.tensor_tensor(xb, MISC.rearrange("p (t c) -> p t c", t=TILES), xb,
                                              ALU.add).then_inc(x1_ready, 1)
                        if s == 8 and maxima:
                            max_low(b + 1, 0)
                        if s == 11 and scores:
                            normalise(b, 0)
                        if s == 1 and ranks:
                            pick_rows(b - 2, u)
                        if s == 8 and tail:
                            wait_alone(dve, m, x1_ready, b)
                            norm_stats(b - 1)
                        if s == 10 and tail:
                            norm(b - 1, n - (1 - u), 1 - u)
                        if s == 14 and tail:
                            logits_shift(b - 1)
                        if s == 15 and tail:
                            choose(b - 1)
                every_graph(body)(dve)
                dve.wait_ge(pos_ready, GRAPHS)

            @block.tensor
            def _(pe):
                pe.wait_ge(ones_ready, 1)

                def body(b, n, u, scores, maxima, tail, ranks):
                    v, nv = 1 - u, n + u
                    for s in range(SLOTS):
                        kt, pair, g = s % HALF // 2, s % 2, s // HALF
                        if scores:
                            buf = 2 * u + g
                            if s % HALF == 0:
                                pe.wait_ge(shift_loaded[buf], 48 * n + 48)
                            pe.wait_ge(st_free[s % 2], HALF * b + s // 2 + 1)
                            for h in (0, 1):
                                hl = 2 * pair + h
                                last = pe.matmul(ST[s % 2][:, h, :],
                                                 ks[0:ROWS + 3, buf, hl, kt * P:(kt + 1) * P],
                                                 qs[0:ROWS + 3, buf, hl, :], start=True, stop=True)
                            last.then_inc(st_ready, 1)
                        if maxima:
                            buf = 2 * v + g
                            i = SLOTS * (b + 1) + s
                            hl, q0 = s % HALF // 2, 2 * (s % 2)
                            if s % HALF == 0:
                                pe.wait_ge(qk_loaded[buf], QK_DMAS * nv + QK_DMAS)
                            wait_pos(pe, max_done, i)
                            for q in (0, 1):
                                last = pe.matmul(SM[:, q, :],
                                                 qs[0:ROWS, buf, hl, (q0 + q) * P:(q0 + q + 1) * P],
                                                 ks[0:ROWS, buf, hl, :], start=True, stop=True)
                            last.then_inc(sm_ready, 1)

                        if s % 2 and (scores if s >= 3 else tail):
                            if s >= 3:
                                vb, vu, vn, t, gg = b, u, n, (s - 3) % HALF // 2, (s - 3) // HALF
                                dve_n = N_DVE * b + dve_made(s - 2)
                                pool_n = N_POOL * b + pool_made(s - 2)
                            else:
                                vb, vu, vn, t, gg = b - 1, 1 - u, n - (1 - u), TILES - 1, 1
                                dve_n, pool_n = N_DVE * b, N_POOL * b
                            if t == 0:
                                wait_pos(pe, osb_ready, 2 * vb + gg)
                                if gg == 0:
                                    pe.wait_ge(v_loaded[vu], 16 * vn + 16)
                            wait_pos(pe, made_dve, dve_n)
                            wait_pos(pe, made_pool, pool_n)
                            for j in range(GROUP):
                                slot = (s - 3 + j // 2) % 4
                                last = pe.matmul(OT[32 * j:32 * j + 32, :],
                                                 vp[:, vu, t, gg * GROUP + j, :], pr[:, slot, j % 2, :],
                                                 start=(t == 0), stop=(t == TILES - 1),
                                                 skip_group_check=True)
                            last.then_inc(pv_done, 1)

                        def turn_max(bb, gg, buf):
                            pe.wait_ge(max_done, SLOTS * bb + HALF * gg + HALF)
                            pe.transpose(MISC[0:16, 0:P], mx[:, buf, :], m.ident[:, :]).then_inc(mt_psum, 1)

                        def turn_values(bb, gg):
                            pe.wait_ge(osb_ready, 2 * bb + gg + 1)
                            for t in range(TILES):
                                last = pe.transpose(MISC[:, t * P:(t + 1) * P], osb[:, t * P:(t + 1) * P],
                                                    m.ident[:, :])
                            last.then_inc(ot_psum, 1)

                        if s == 0 and scores:
                            if tail:
                                wait_pos(pe, an_ready, 2 * b - 1)
                                wait_pos(pe, lg_read, b - 1)
                            turn_max(b, 1, 2 * u + 1)
                        if s == 1 and ranks:
                            if scores:
                                pe.wait_ge(mt_rest, 2 * b + 2)
                            pe.wait_ge(given_ready, b - 1)
                            rk = MISC[:, 0:TILES * EXPERTS]
                            pe.matmul(rk, m.before[:, :], given[:, :, :].rearrange("p t e -> p (t e)"),
                                      start=True, stop=False)
                            pe.matmul(rk, m.ones[:, :],
                                      m.counts[:, 0:TILES, :].rearrange("p t e -> p (t e)"),
                                      start=False, stop=True).then_inc(rank_psum, 1)
                        if s == 2 and tail:
                            if scores:
                                pe.wait_ge(mt_rest, 2 * b + 2)
                            if ranks:
                                pe.wait_ge(rank_read, b - 1)
                            turn_values(b - 1, 1)
                        if s == 4 and tail:
                            pe.wait_ge(an_ready, 2 * b)
                            for t in range(TILES):
                                last = pe.transpose(MISC[:, t * P:(t + 1) * P], an[:, t, :], m.ident[:, :])
                            last.then_inc(at_psum, 1)
                        if s == 6 and tail:
                            pe.wait_ge(at_ready, b)
                            for t in range(TILES):
                                last = pe.matmul(MISC[:, t * P:(t + 1) * P], anT[:, t * P:(t + 1) * P],
                                                 m.wo[:, :], start=True, stop=True)
                            last.then_inc(wo_psum, 1)
                        if s == 8 and maxima:
                            wait_pos(pe, x1_ready, b)
                            turn_max(b + 1, 0, 2 * v)
                        if s == 10 and scores:
                            if maxima:
                                pe.wait_ge(mt_rest, 2 * b + 3)
                            else:
                                pe.wait_ge(x1_ready, b)
                            turn_values(b, 0)
                        if s == 12 and tail:
                            if scores:
                                pe.wait_ge(an_ready, 2 * b + 1)
                            pe.wait_ge(xn_ready, b)
                            wait_pos(pe, x1_ready, b)
                            for t in range(TILES):
                                last = pe.transpose(MISC[:, t * P:(t + 1) * P], xn[:, 1 - u, t, :],
                                                    m.ident[:, :])
                            last.then_inc(xnT_psum, 1)
                        if s == 13 and tail:
                            pe.wait_ge(xnT_ready, b)
                            for t in range(TILES):
                                last = pe.matmul(MISC[:, t * EXPERTS:(t + 1) * EXPERTS],
                                                 xnT[:, t * P:(t + 1) * P], m.router[:, :],
                                                 start=True, stop=True)
                            last.then_inc(lg_psum, 1)
                every_graph(body)(pe)


def stage_experts(nc, m, w13_d, w2_d, rows_d, outs_d, out_d):
    I32, U32 = mybir.dt.int32, mybir.dt.uint32
    SHIFT = BLOCK.bit_length() - 1
    with ExitStack() as ctx:
        def sb(name, shape, dt=F32):
            return ctx.enter_context(nc.sbuf_tensor(name, shape, dt))

        def sem(name):
            return ctx.enter_context(nc.semaphore(name))

        E, NB = EXPERTS, N_BLOCKS
        zeros = sb("zero_rows", [P, SUB, HID])
        count = sb("expert_count", [P, E])
        full = sb("expert_blocks_int", [P, 2, E], I32)
        many = sb("expert_blocks", [P, E])
        none = sb("no_blocks", [P, E])
        last_b = sb("blocks_up_to", [P, E])
        first_b = sb("first_block", [P, E])
        CH = GRAPHS * TILES * TOP
        move = sb("region_to_block", [P, E])
        mine = sb("my_expert", [P, CH, E])
        moved = sb("my_move", [P, CH])
        past = sb("past_expert", [1, NB, E])
        begun = sb("begun_expert", [1, NB, E])
        where = sb("row_if_expert", [1, NB, E])
        number = sb("expert_of_block_f", [1, NB])
        spill = sb("is_trash", [1, NB])
        src_f, end_f = sb("read_row_f", [1, NB]), sb("end_row_f", [1, E])
        exp_i, src_i, end_i = (sb(n, [1, NB], U32) for n in ("expert_of_block", "read_row", "end_row"))
        xr = sb("block_rows", [P, 2, SUB, HID])
        xT = sb("block_T", [P, 2, BLOCK])
        w13 = sb("w13_block", [P, 2, 2, FT, P])
        w2 = sb("w2_block", [P, 2, FT, HID])
        act1 = sb("silu_h1", [P, 2, FT, BLOCK])
        hid = sb("hidden", [P, 2, FT, BLOCK])
        yr = sb("block_out", [P, 2, SUB, HID])

        z_ready, cnt_psum, tab_chain, tab_ready = (sem(n) for n in (
            "zero_rows_ready", "counts_summed", "table_chain", "table_ready"))
        ends = sem("region_ends_zeroed")
        loaded = [sem("block_loaded0"), sem("block_loaded1")]
        xT_psum, xT_ready, h_psum, act_ready, hid_ready, y_psum, y_ready = (sem(n) for n in (
            "block_turned", "block_T_ready", "h_ready", "silu_ready", "hidden_ready", "y_summed", "y_ready"))
        y_out = [sem("block_stored0"), sem("block_stored1")]

        H = [m.psum[:, 0:FT, :], m.psum[:, FT:2 * FT, :]]
        XT, Y = m.psum[:, 6, :], m.psum[:, 7, :]

        with nc.Block() as block:
            @block.gpsimd
            def _(pool):
                pool.memset(zeros[:, :, :], 0.0).then_inc(z_ready, 1)

            @block.vector
            def _(dve):
                ch = Chain(dve, tab_chain, 0)
                L = ch.link
                dve.wait_ge(cnt_psum, 1)
                L(dve.tensor_copy(count[:, :], m.psum[:, 7, 0:E]))
                L(dve.tensor_scalar_add(full[:, 0, :], count[:, :], float(BLOCK - 1)))
                L(dve.tensor_single_scalar(full[:, 1, :], full[:, 0, :], SHIFT, ALU.arith_shift_right))
                L(dve.tensor_copy(many[:, :], full[:, 1, :]))
                L(dve.memset(none[:, :], 0.0))
                L(dve.tensor_tensor_scan(last_b[:, :], many[:, :], none[:, :], 0.0, ALU.add, ALU.add))
                L(dve.tensor_tensor(first_b[:, :], last_b[:, :], many[:, :], ALU.subtract))
                L(dve.tensor_tensor(end_f[:, :], m.small[0:1, E:2 * E], count[0:1, :], ALU.add))
                L(dve.tensor_copy(end_i[:, 0:E], end_f[:, :]))
                nb = m.blocks[0:1, :].unsqueeze(2).to_broadcast([1, NB, E])

                def per_expert(a):
                    return a.unsqueeze(1).to_broadcast([1, NB, E])
                L(dve.tensor_tensor(past[:, :, :], nb, per_expert(last_b[0:1, :]), ALU.is_ge))
                L(dve.tensor_tensor(begun[:, :, :], nb, per_expert(first_b[0:1, :]), ALU.is_ge))
                L(dve.tensor_tensor(begun[:, :, :], begun[:, :, :], past[:, :, :], ALU.subtract))
                L(dve.tensor_reduce(number[:, :], past[:, :, :], AX.X, ALU.add))
                L(dve.tensor_tensor(where[:, :, :], nb, per_expert(first_b[0:1, :]), ALU.subtract))
                L(dve.tensor_scalar(where[:, :, :], where[:, :, :], float(BLOCK), None, ALU.mult))
                L(dve.tensor_tensor(where[:, :, :], where[:, :, :], per_expert(m.small[0:1, E:2 * E]), ALU.add))
                L(dve.tensor_tensor(where[:, :, :], where[:, :, :], begun[:, :, :], ALU.mult))
                L(dve.tensor_reduce(src_f[:, :], where[:, :, :], AX.X, ALU.add))
                L(dve.tensor_scalar(spill[:, :], number[:, :], float(E), float(TRASH), ALU.is_ge, ALU.mult))
                L(dve.tensor_tensor(src_f[:, :], src_f[:, :], spill[:, :], ALU.add))
                L(dve.tensor_scalar(number[:, :], number[:, :], float(E - 1), None, ALU.min))
                L(dve.tensor_copy(exp_i[:, :], number[:, :]))
                dve.tensor_copy(src_i[:, :], src_f[:, :]).then_inc(tab_ready, 1)
                L(dve.tensor_scalar(move[:, :], first_b[:, :], float(BLOCK), None, ALU.mult))
                L(dve.tensor_tensor(move[:, :], move[:, :], m.small[:, E:2 * E], ALU.subtract))
                pos = m.pos[:, :, :].rearrange("p t k -> p (t k)")
                L(dve.tensor_tensor(mine[:, :, :],
                                    m.chosen[:, :, :].rearrange("p t k -> p (t k)").unsqueeze(2)
                                    .to_broadcast([P, CH, E]),
                                    m.small[:, 0:E].unsqueeze(1).to_broadcast([P, CH, E]), ALU.is_equal))
                L(dve.tensor_tensor(mine[:, :, :], mine[:, :, :],
                                    move[:, :].unsqueeze(1).to_broadcast([P, CH, E]), ALU.mult))
                L(dve.tensor_reduce(moved[:, :], mine[:, :, :], AX.X, ALU.add))
                L(dve.tensor_tensor(pos, pos, moved[:, :], ALU.add))

                dve.sem_inc(hid_ready, 2)
                dve.sem_inc(act_ready, 2)

                def body(i, u):
                    j = 2 * i + u
                    dve.wait_ge(act_ready, j + 1 + 2)
                    dve.wait_ge(y_psum, j + 1)
                    dve.tensor_tensor(hid[:, u, :, :], act1[:, u, :, :], H[u][:, :, BLOCK:2 * BLOCK],
                                      ALU.mult).then_inc(hid_ready, 1)
                with dve.Fori(0, NB // 2) as i:
                    for u in (0, 1):
                        body(i, u)

            @block.sync
            def _(sp):
                sp.wait_ge(z_ready, 1)
                sp.wait_ge(tab_ready, 1)

                def zero_rows(row):
                    sp.dma_start(rows_d[bass.ds(row, BLOCK), :].rearrange("(p s) c -> p s c", s=SUB),
                                 zeros[:, :, :]).then_inc(ends, 16)
                for e in range(E):
                    r = sp.value_load(end_i[0:1, e:e + 1], min_val=0, max_val=TRASH - BLOCK)
                    zero_rows(r)
                zero_rows(TRASH)
                sp.wait_ge(ends, 16 * (E + 1))

                def body(i, u):
                    j = 2 * i + u
                    sp.wait_ge(y_psum, j + 1)
                    r = sp.value_load(src_i[0:1, bass.ds(j, 1)], min_val=0, max_val=TRASH)
                    e = sp.value_load(exp_i[0:1, bass.ds(j, 1)], min_val=0, max_val=E - 1)
                    sp.dma_start(xr[:, u, :, :], rows_d[bass.ds(r, BLOCK), :].rearrange(
                        "(p s) c -> p s c", s=SUB)).then_inc(loaded[u], 16)
                    sp.dma_start(w13[:, u, :, :, :].rearrange("p a t h -> p (a t h)"),
                                 w13_d[bass.ds(e, 1), :, :].squeeze(0)).then_inc(loaded[u], 16)
                    sp.dma_start(w2[:, u, :, :].rearrange("p t c -> p (t c)"),
                                 w2_d[bass.ds(e, 1), :, :].squeeze(0)).then_inc(loaded[u], 16)
                with sp.Fori(0, NB // 2) as i:
                    for u in (0, 1):
                        body(i, u)

            @block.tensor
            def _(pe):
                pe.matmul(m.psum[:, 7, 0:E], m.ones[:, :], m.counts[:, TILES, :],
                          start=True, stop=True).then_inc(cnt_psum, 1)
                pe.wait_ge(tab_ready, 1)
                pe.sem_inc(y_psum, 2)
                pe.wait_ge(hid_ready, 2)

                def body(i, u):
                    j = 2 * i + u
                    pe.wait_ge(loaded[u], 48 * i + 48)
                    pe.wait_ge(xT_ready, j + 1)
                    for t in range(SUB):
                        last = pe.transpose(XT[:, t * P:(t + 1) * P], xr[:, u, t, :], m.ident[:, :])
                    last.then_inc(xT_psum, 1)
                    pe.wait_ge(xT_ready, j + 1 + 1)
                    pe.wait_ge(hid_ready, j + 1)
                    for t in range(FT):
                        for a in (0, 1):
                            last = pe.matmul(H[u][:, t, a * BLOCK:(a + 1) * BLOCK], w13[:, u, a, t, :],
                                             xT[:, u, :], start=True, stop=True)
                    last.then_inc(h_psum, 1)
                    pe.wait_ge(hid_ready, j + 1 + 2)
                    pe.wait_ge(y_ready, j + 1)
                    for r in range(SUB):
                        for t in range(FT):
                            last = pe.matmul(Y[:, r * P:(r + 1) * P], hid[:, u, t, r * P:(r + 1) * P],
                                             w2[:, u, t, :], start=(t == 0), stop=(t == FT - 1))
                    last.then_inc(y_psum, 1)
                with pe.Fori(0, NB // 2) as i:
                    for u in (0, 1):
                        body(i, u)

            @block.scalar
            def _(act):
                act.sem_inc(xT_ready, 1)
                act.sem_inc(y_ready, 1)
                for u in (0, 1):
                    act.sem_inc(y_out[u], 16)

                def body(i, u):
                    j = 2 * i + u
                    act.wait_ge(xT_psum, j + 1)
                    act.wait_ge(h_psum, j + 1)
                    act.copy(xT[:, u, :], XT[:, 0:BLOCK]).then_inc(xT_ready, 1)
                    act.wait_ge(h_psum, j + 1 + 2)
                    act.wait_ge(hid_ready, j + 1)
                    act.activation(act1[:, u, :, :], H[u][:, :, 0:BLOCK], ACT.Silu).then_inc(act_ready, 1)
                    act.wait_ge(y_psum, j + 1 + 2)
                    act.wait_ge(y_out[u], 16 * i + 16)
                    act.copy(yr[:, u, :, :], Y[:, 0:SUB * HID].rearrange("p (s c) -> p s c", s=SUB)
                             ).then_inc(y_ready, 1)
                    act.wait_ge(y_ready, j + 1 + 1)
                    act.dma_start(outs_d[bass.ds(j * BLOCK, BLOCK), :].rearrange("(p s) c -> p s c", s=SUB),
                                  yr[:, u, :, :]).then_inc(y_out[u], 16)
                act.sem_inc(h_psum, 2)
                with act.Fori(0, NB // 2) as i:
                    for u in (0, 1):
                        body(i, u)
                for u in (0, 1):
                    act.wait_ge(y_out[u], 16 + 16 * (NB // 2))


def stage_combine(nc, m, outs_d, out_d):
    with ExitStack() as ctx:
        def sb(name, shape, dt=F32):
            return ctx.enter_context(nc.sbuf_tensor(name, shape, dt))

        def sem(name):
            return ctx.enter_context(nc.semaphore(name))

        idx = sb("rows_of_graph", [P, 2, TILES, TOP], mybir.dt.uint32)
        got = sb("gathered", [P, 2, TILES, TOP, HID])
        res = sb("result", [P, 2, TILES, HID])
        idx_ready, got_ready = sem("index_ready"), [sem("gathered0"), sem("gathered1")]
        half_sum, res_ready, stored = sem("first_added"), sem("result_ready"), [sem("stored0"), sem("stored1")]
        G = 16 * TILES * TOP

        with nc.Block() as block:
            @block.gpsimd
            def _(pool):
                def body(n, u):
                    b = 2 * n + u
                    wait_alone(pool, m, idx_ready, b + 1)
                    wait_alone(pool, m, res_ready, b + 1)
                    for t in range(TILES):
                        for k in range(TOP):
                            pool.indirect_dma_start(
                                got[:, u, t, k, :], None, outs_d[:, :],
                                bass.IndirectOffsetOnAxis(ap=idx[:, u, t, k:k + 1], axis=0)
                            ).then_inc(got_ready[u], 16)
                with pool.Fori(0, GRAPHS // 2) as n:
                    for u in (0, 1):
                        body(n, u)

            @block.vector
            def _(dve):
                dve.sem_inc(res_ready, 2)

                def index(b, u, n):
                    dve.tensor_copy(idx[:, u, :, :], m.pos[:, bass.ds(b * TILES, TILES), :]
                                    ).then_inc(idx_ready, 1)

                def add(n, u):
                    b = 2 * n + u
                    dve.wait_ge(got_ready[u], G * (n + 1))
                    dve.wait_ge(stored[u], 16 * n + 16)
                    for t in range(TILES):
                        last = dve.scalar_tensor_tensor(res[:, u, t, :], got[:, u, t, 0, :],
                                                        m.gates[:, b * TILES + t, 0:1],
                                                        m.x[:, b * TILES + t, :], ALU.mult, ALU.add)
                    last.then_inc(half_sum, 1)
                    dve.wait_ge(half_sum, b + 1)
                    for t in range(TILES):
                        last = dve.scalar_tensor_tensor(res[:, u, t, :], got[:, u, t, 1, :],
                                                        m.gates[:, b * TILES + t, 1:2],
                                                        res[:, u, t, :], ALU.mult, ALU.add)
                    last.then_inc(res_ready, 1)

                index(0, 0, 0)
                index(1, 1, 0)
                with dve.Fori(0, GRAPHS // 2 - 1) as n:
                    for u in (0, 1):
                        add(n, u)
                        index(2 * n + u + 2, u, n)
                for u in (0, 1):
                    add(GRAPHS // 2 - 1, u)

            @block.sync
            def _(sp):
                for u in (0, 1):
                    sp.sem_inc(stored[u], 16)

                def body(n, u):
                    b = 2 * n + u
                    sp.wait_ge(res_ready, b + 1 + 2)
                    sp.dma_start(out_d[b, :, :].rearrange("(t p) c -> p t c", p=P), res[:, u, :, :]
                                 ).then_inc(stored[u], 16)
                with sp.Fori(0, GRAPHS // 2) as n:
                    for u in (0, 1):
                        body(n, u)
                for u in (0, 1):
                    sp.wait_ge(stored[u], 16 + 16 * (GRAPHS // 2))


def build(nc, x, adjT, wq, wk, wv, wo, bo, router, before, small, blocks, w13, w2, out):
    with ExitStack() as ctx:
        m = place(nc, ctx)
        qk = nc.dram_tensor("qk_parts_dram", [GRAPHS, 6, P, NODES], BF16).ap()
        v = nc.dram_tensor("v_padded_dram", [GRAPHS, P, TILES * HEADS * 32], F32).ap()
        rows = nc.dram_tensor("rows_by_expert", [TRASH + BLOCK, HID], F32).ap()
        outs = nc.dram_tensor("outs_by_block", [N_BLOCKS * BLOCK, HID], F32).ap()
        stage_projections(nc, m, x, (wq, wk, wv, wo, bo, router, before, small, blocks), qk, v)
        stage_attention(nc, m, adjT, qk, v, rows)
        stage_experts(nc, m, w13, w2, rows, outs, out)
        stage_combine(nc, m, outs, out)


def layout(x, adj, Wq, Wk, Wv, Wo, bo, router_w, w1, w2, w3):
    import numpy as np

    c = np.ascontiguousarray
    by_place = np.arange(HID).reshape(HEADS, DH).T.reshape(-1)
    w13 = np.zeros((EXPERTS, HID, 2, FT * P), np.float32)
    w13[:, :, 0, :FFN] = w1.transpose(0, 2, 1)
    w13[:, :, 1, :FFN] = w3.transpose(0, 2, 1)
    w2p = np.zeros((EXPERTS, FT * P, HID), np.float32)
    w2p[:, :FFN, :] = w2.transpose(0, 2, 1)
    small = np.concatenate([np.arange(EXPERTS), np.arange(EXPERTS) * REGION]).astype(np.float32)
    return {
        "x": c(x), "adjT": c(adj.transpose(0, 2, 1)),
        "wq": c(Wq[by_place].T), "wk": c(Wk[by_place].T), "wv": c(Wv.T), "wo": c(Wo.T),
        "bo": c(np.broadcast_to(bo, (P, HID))), "router": c(router_w.T),
        "before": np.triu(np.ones((P, P), np.float32), 1),
        "small": c(np.broadcast_to(small, (P, 2 * EXPERTS))),
        "blocks": c(np.broadcast_to(np.arange(N_BLOCKS, dtype=np.float32), (P, N_BLOCKS))),
        "w13": w13.reshape(EXPERTS, HID, 2 * FT * P),
        "w2": c(w2p.reshape(EXPERTS, FT, P, HID).transpose(0, 2, 1, 3)).reshape(EXPERTS, P, FT * HID),
    }


def kernel(x, adj, L0_gnn_Wq, L0_gnn_Wk, L0_gnn_Wv, L0_gnn_Wo, L0_gnn_bo, L0_ffn_router_w,
           L0_ffn_w1, L0_ffn_w2, L0_ffn_w3):
    import numpy as np
    import concourse.bacc as bacc
    from concourse.bass_utils import run_bass_kernel_spmd

    given = (x, adj, L0_gnn_Wq, L0_gnn_Wk, L0_gnn_Wv, L0_gnn_Wo, L0_gnn_bo, L0_ffn_router_w,
             L0_ffn_w1, L0_ffn_w2, L0_ffn_w3)
    arrays = layout(*(np.asarray(a) for a in given))
    nc = bacc.Bacc("TRN2", target_bir_lowering=False, num_devices=1)
    args = {k: nc.dram_tensor(k, a.shape, mybir.dt.from_np(a.dtype), kind="ExternalInput").ap()
            for k, a in arrays.items()}
    out = nc.dram_tensor("out", (GRAPHS, NODES, HID), F32, kind="ExternalOutput").ap()
    build(nc, **args, out=out)
    r = run_bass_kernel_spmd(nc, [arrays], core_ids=[0])
    return r.results[0]["out"]
```

```python
import concourse.bass as bass
from concourse import mybir
from contextlib import ExitStack

F32 = mybir.dt.float32
BF16 = mybir.dt.bfloat16
ALU = mybir.AluOpType
ACT = mybir.ActivationFunctionType
AX = mybir.AxisListType

P = 128
GRAPHS, NODES, HID = 16, 512, 128
HEADS = 8
DH = HID // HEADS
TILES = NODES // P
SLOTS = 16
HALF = SLOTS // 2
GROUP = HEADS // 2
Q_PARTS = (0, 0, 0, 1, 1, 2)
K_PARTS = (0, 1, 2, 0, 1, 0)
ROWS = len(Q_PARTS) * DH
QK_DMAS = 16 * 2 * len(Q_PARTS)
ADJ_EPS = 1e-6
LN_EPS = 1e-5
EXPERTS, TOP = 8, 2
FFN = 341
FT = -(-FFN // P)
TOKENS = GRAPHS * NODES
BLOCK = 256
SUB = BLOCK // P
REGION = TOKENS + BLOCK
N_BLOCKS = TOP * TOKENS // BLOCK + EXPERTS
TRASH = EXPERTS * REGION
DEEP = 4
FIRST, TOKEN = HID, HID + 1
WIDE = HID + 2
CONSTANTS = 9
POOL_SLOTS = (1, 4, 7, 10, 13)
N_POOL = len(POOL_SLOTS)
N_DVE = SLOTS - N_POOL


def pool_made(s):
    return sum(1 for x in POOL_SLOTS if x <= s)


def dve_made(s):
    return s + 1 - pool_made(s)


def wait_alone(eng, m, sem, value):
    if not isinstance(value, int):
        value = eng.to_reg(value)
    if not isinstance(value, int) or value > 0:
        eng.wait_ge(m.ident_ready, 1)
        eng.wait_ge(sem, value)


def wait_pos(eng, s, value):
    if not isinstance(value, int) or value > 0:
        eng.wait_ge(s, value)


class Chain:

    def __init__(self, eng, sem, base):
        self.eng, self.sem, self.base, self.n = eng, sem, base, 0

    def link(self, ins, m=None):
        self.n += 1
        ins.then_inc(self.sem, 1)
        if m is None:
            self.eng.wait_ge(self.sem, self.base + self.n)
        else:
            wait_alone(self.eng, m, self.sem, self.base + self.n)


class Memory:
    pass


def place(nc, ctx):
    m = Memory()

    def sb(name, shape, dt=F32):
        return ctx.enter_context(nc.sbuf_tensor(name, shape, dt))

    def sem(name):
        return ctx.enter_context(nc.semaphore(name))

    m.x = sb("x_all", [P, GRAPHS * TILES, HID])
    m.ident = sb("ident", [P, P])
    m.wq, m.wk, m.wv, m.wo = (sb(n, [P, HID]) for n in ("wqT", "wkT", "wvT", "woT"))
    m.bo = sb("bo_rows", [P, HID])
    m.router = sb("routerT", [P, EXPERTS])
    m.before = sb("before_me", [P, P])
    m.ones = sb("all_ones", [P, P])
    m.small = sb("small_constants", [P, 2 * EXPERTS + TILES])
    m.blocks = sb("block_numbers", [P, N_BLOCKS])
    m.gates = sb("gates", [P, GRAPHS * TILES, TOP])
    m.counts = sb("seen_before", [P, TILES + 1, EXPERTS])
    m.psum = ctx.enter_context(nc.psum_tensor("psum", [P, 8, 512], F32))
    m.sb, m.sem = sb, sem
    m.const_in = sem("const_in")
    m.ident_ready = sem("ident_ready")
    return m


def stage_projections(nc, m, x_d, w_d, qk_d, v_d):
    with ExitStack() as ctx:
        def sb(name, shape, dt=F32):
            return ctx.enter_context(nc.sbuf_tensor(name, shape, dt))

        def sem(name):
            return ctx.enter_context(nc.semaphore(name))

        stats = sb("ln_stats", [P, 2, TILES, 6])
        mv = sb("ln_mean_var", [P, 2, TILES, 2])
        var_eps = sb("ln_var_eps", [P, 2, TILES])
        minus_half = sb("minus_half", [P, TILES])
        rstd = sb("ln_rstd", [P, 2, TILES])
        xn = sb("xn", [P, 2, TILES, HID])
        xnT = sb("xnT", [P, 2, NODES])
        parts = sb("qk_parts", [P, 2, 6, NODES], BF16)
        rest = sb("qk_rest", [P, 2, 2, NODES])
        vpad = sb("v_padded", [P, 2, TILES, HEADS, 32])

        x_in = [sem("x_in0"), sem("x_in1")]
        half_ready, var_ready, rstd_ready = sem("half_ready"), sem("var_ready"), sem("rstd_ready")
        xn_ready, xnT_psum, xnT_ready = sem("xn_ready"), sem("xnT_psum"), sem("xnT_ready")
        q_psum, k_psum, v_psum = sem("q_psum"), sem("k_psum"), sem("v_psum")
        high_ready, rest_ready, mid_ready = sem("high_ready"), sem("rest_ready"), sem("mid_ready")
        low_ready, v_ready, vpad_init = sem("low_ready"), sem("v_ready"), sem("vpad_init")
        biased = sem("residual_biased")
        stored = [sem("stacks_stored0"), sem("stacks_stored1")]
        dve_chain = sem("s1_dve_chain")
        DVE_LINKS = 2

        def rounds(eng, body):
            with eng.Fori(0, GRAPHS // 2) as n:
                for u in (0, 1):
                    body(n, u)

        with nc.Block() as block:
            @block.sync
            def _(sp):
                for t, d in ((m.wq, w_d[0]), (m.wk, w_d[1]), (m.wv, w_d[2]), (m.wo, w_d[3])):
                    sp.dma_start(t[:, :], d).then_inc(m.const_in, 16)
                for t, d in ((m.bo, w_d[4]), (m.router, w_d[5]), (m.before, w_d[6]),
                             (m.small, w_d[7]), (m.blocks, w_d[8])):
                    sp.dma_start(t[:, :], d).then_inc(m.const_in, 16)

                def loads(n, u):
                    b = 2 * n + u
                    sp.wait_ge(xn_ready, b + 1)
                    sp.dma_start(m.x[:, bass.ds(b * TILES, TILES), :],
                                 x_d[b, :, :].rearrange("(t p) c -> p t c", p=P)).then_inc(x_in[u], 16)
                rounds(sp, loads)
                for u in (0, 1):
                    sp.wait_ge(stored[u], 32 * (GRAPHS // 2) + 32)

            @block.gpsimd
            def _(pool):
                pool.memset(m.ident[:, :], 0.0).then_inc(m.ident_ready, 1)
                pool.wait_ge(m.ident_ready, 1)
                pool.affine_select(out=m.ident[:, :], in_=m.ident[:, :], compare_op=ALU.not_equal,
                                   fill=1.0, base=0, pattern=[[-1, P]], channel_multiplier=1
                                   ).then_inc(m.ident_ready, 1)
                pool.memset(m.ones[:, :], 1.0).then_inc(half_ready, 1)
                pool.memset(m.counts[:, :, :], 0.0).then_inc(half_ready, 1)
                pool.memset(minus_half[:, :], -0.5).then_inc(half_ready, 1)
                pool.wait_ge(half_ready, 3)
                pool.memset(vpad[:, :, :, :, :], 0.0).then_inc(vpad_init, 1)
                pool.wait_ge(vpad_init, 1)
                pool.memset(vpad[:, :, :, :, DH:DH + 1], 1.0).then_inc(vpad_init, 1)
                pool.wait_ge(m.const_in, CONSTANTS * 16)

                def invert(n, u):
                    b = 2 * n + u
                    pool.wait_ge(var_ready, b + 1)
                    pool.tensor_tensor(rstd[:, u, :], var_eps[:, u, :], minus_half[:, :],
                                       ALU.pow).then_inc(rstd_ready, 1)

                def low(n, u):
                    b = 2 * n + u
                    for j in range(2):
                        pool.wait_ge(mid_ready, 2 * b + j + 1)
                        pool.tensor_tensor(parts[:, u, 3 * j + 2, :], rest[:, u, j, :],
                                           parts[:, u, 3 * j + 1, :], ALU.subtract).then_inc(low_ready, 1)
                    xb = m.x[:, bass.ds(b * TILES, TILES), :]
                    pool.tensor_tensor(xb, xb, m.bo[:, :].unsqueeze(1).to_broadcast([P, TILES, HID]),
                                       ALU.add).then_inc(biased, 1)

                invert(0, 0)
                with pool.Fori(0, GRAPHS // 2 - 1) as n:
                    invert(n, 1)
                    low(n, 0)
                    invert(n + 1, 0)
                    low(n, 1)
                invert(GRAPHS // 2 - 1, 1)
                low(GRAPHS // 2 - 1, 0)
                low(GRAPHS // 2 - 1, 1)
                pool.wait_ge(biased, GRAPHS)

            @block.vector
            def _(dve):
                dve.sem_inc(xn_ready, 2)

                def norm(n, u):
                    b = 2 * n + u
                    c = Chain(dve, dve_chain, DVE_LINKS * b)
                    wait_alone(dve, m, x_in[u], 16 * (n + 1))
                    for t in range(TILES):
                        last = dve.bn_stats(stats[:, u, t, :], m.x[:, b * TILES + t, :])
                    c.link(last, m)
                    for t in range(TILES):
                        last = dve.bn_aggr(mv[:, u, t, :], stats[:, u, t, :])
                    c.link(last)
                    dve.tensor_scalar_add(var_eps[:, u, :], mv[:, u, :, 1], LN_EPS).then_inc(var_ready, 1)
                    dve.wait_ge(rstd_ready, b + 1)
                    dve.wait_ge(xnT_psum, b + 1)
                    for t in range(TILES):
                        last = dve.tensor_scalar(xn[:, u, t, :], m.x[:, b * TILES + t, :],
                                                 mv[:, u, t, 0:1], rstd[:, u, t:t + 1],
                                                 ALU.subtract, ALU.mult)
                    last.then_inc(xn_ready, 1)

                def split(n, u):
                    b = 2 * n + u
                    for j in range(2):
                        dve.wait_ge(high_ready, 2 * b + j + 1)
                        dve.wait_ge(low_ready, 2 * b + j + 1)
                        dve.tensor_tensor(rest[:, u, j, :], m.psum[:, 2 + 2 * j + u, :],
                                          parts[:, u, 3 * j, :], ALU.subtract).then_inc(rest_ready, 1)
                        dve.wait_ge(rest_ready, 2 * b + j + 1 + 4)
                        dve.tensor_copy(parts[:, u, 3 * j + 1, :], rest[:, u, j, :]).then_inc(mid_ready, 1)

                dve.sem_inc(low_ready, 4)
                dve.sem_inc(rest_ready, 4)
                dve.sem_inc(xnT_psum, 2)
                norm(0, 0)
                with dve.Fori(0, GRAPHS // 2 - 1) as n:
                    norm(n, 1)
                    split(n, 0)
                    norm(n + 1, 0)
                    split(n, 1)
                norm(GRAPHS // 2 - 1, 1)
                split(GRAPHS // 2 - 1, 0)
                split(GRAPHS // 2 - 1, 1)

            @block.tensor
            def _(pe):
                pe.wait_ge(m.ident_ready, 2)
                pe.wait_ge(m.const_in, CONSTANTS * 16)

                def body(n, u):
                    b = 2 * n + u
                    pe.wait_ge(xn_ready, b + 1 + 2)
                    pe.wait_ge(xnT_ready, b + 1)
                    for t in range(TILES):
                        last = pe.transpose(m.psum[:, u, t * P:(t + 1) * P], xn[:, u, t, :], m.ident[:, :])
                    last.then_inc(xnT_psum, 1)
                    pe.wait_ge(xnT_ready, b + 1 + 2)
                    pe.wait_ge(rest_ready, 2 * b + 1)
                    pe.matmul(m.psum[:, 2 + u, :], m.wq[:, :], xnT[:, u, :],
                              start=True, stop=True).then_inc(q_psum, 1)
                    pe.wait_ge(rest_ready, 2 * b + 2)
                    pe.matmul(m.psum[:, 4 + u, :], m.wk[:, :], xnT[:, u, :],
                              start=True, stop=True).then_inc(k_psum, 1)
                    pe.wait_ge(v_ready, b + 1)
                    for t in range(TILES):
                        last = pe.matmul(m.psum[:, 6 + u, t * P:(t + 1) * P],
                                         xnT[:, u, t * P:(t + 1) * P], m.wv[:, :], start=True, stop=True)
                    last.then_inc(v_psum, 1)
                rounds(pe, body)

            @block.scalar
            def _(act):
                act.sem_inc(xnT_ready, 2)
                act.sem_inc(v_ready, 2)
                act.sem_inc(stored[0], 32)
                act.sem_inc(stored[1], 32)
                act.wait_ge(vpad_init, 2)

                def body(n, u):
                    b = 2 * n + u
                    act.wait_ge(xnT_psum, b + 1 + 2)
                    act.wait_ge(v_psum, b + 1)
                    act.copy(xnT[:, u, :], m.psum[:, u, :]).then_inc(xnT_ready, 1)
                    act.wait_ge(stored[u], 32 * n + 32)
                    act.wait_ge(q_psum, b + 1)
                    act.copy(parts[:, u, 0, :], m.psum[:, 2 + u, :]).then_inc(high_ready, 1)
                    act.wait_ge(k_psum, b + 1)
                    act.copy(parts[:, u, 3, :], m.psum[:, 4 + u, :]).then_inc(high_ready, 1)
                    act.wait_ge(v_psum, b + 1 + 2)
                    act.copy(vpad[:, u, :, :, 0:DH],
                             m.psum[:, 6 + u, :].rearrange("p (t h d) -> p t h d", t=TILES, h=HEADS)
                             ).then_inc(v_ready, 1)
                    act.wait_ge(v_ready, b + 1 + 2)
                    act.dma_start(v_d[b, :, :], vpad[:, u, :, :, :].rearrange("p t h c -> p (t h c)")
                                  ).then_inc(stored[u], 16)
                    act.wait_ge(low_ready, 2 * b + 2 + 4)
                    act.dma_start(qk_d[b, :, :, :].rearrange("s p c -> p s c"),
                                  parts[:, u, :, :]).then_inc(stored[u], 16)
                act.sem_inc(v_psum, 2)
                rounds(act, body)


def stage_attention(nc, m, adj_d, qk_d, v_d, rows_d):
    with ExitStack() as ctx:
        def sb(name, shape, dt=F32):
            return ctx.enter_context(nc.sbuf_tensor(name, shape, dt))

        def sem(name):
            return ctx.enter_context(nc.semaphore(name))

        qs = sb("q_stack", [P, 4, GROUP, NODES], BF16)
        ks = sb("k_stack", [P, 4, GROUP, NODES], BF16)
        vp = sb("v_pad", [P, 2, TILES, HEADS, 32])
        adj = sb("adj_T", [P, 2, TILES, NODES])
        ex = sb("exp_for_pool", [P, 2, 2, NODES])
        pr = sb("products", [P, 4, 2, NODES])
        mx = sb("minus_max", [P, 4, 16])
        mx_parts = sb("minus_max_parts", [16, 2, 3, P], BF16)
        mx_rest = sb("minus_max_rest", [16, 2, P])
        osb = sb("values_T", [P, NODES])
        rec = sb("row_sum_inverse", [P, TILES, GROUP])
        an = sb("attended", [P, TILES, HID])
        anT = sb("attended_T", [P, NODES])

        stats = sb("ln2_stats", [P, TILES, 6])
        mv = sb("ln2_mean_var", [P, TILES, 2])
        var_eps = sb("ln2_var_eps", [P, TILES])
        minus_half = sb("ln2_minus_half", [P, TILES])
        rstd = sb("ln2_rstd", [P, TILES])
        xn = sb("xn2", [P, 2, TILES, WIDE])
        xnT = sb("xn2_T", [P, NODES])
        lmax = sb("minus_max_logit", [P, TILES])
        prob = sb("router_probs", [P, TILES, EXPERTS])
        psum_inv = sb("prob_sum", [P, 2, TILES])
        top = sb("top_probs", [P, TILES, 8])
        topi = sb("top_experts", [P, TILES, 8], mybir.dt.uint32)
        topf = sb("chosen_experts", [P, TILES, TOP])
        tsum = sb("top_sum", [P, 2, TILES])
        hot = sb("choice_one_hot", [P, TILES, TOP, EXPERTS])
        given = sb("given_to", [P, TILES, EXPERTS])
        rank = sb("rank_rows", [P, TILES, EXPERTS])
        picked = sb("rank_picked", [P, TILES, TOP, EXPERTS])
        posf = sb("row_float", [P, TILES, TOP])
        pos2 = sb("row_index", [P, 2, TILES, TOP], mybir.dt.uint32)

        var_ready, rstd_ready, xn_ready = sem("ln2_var_ready"), sem("ln2_rstd_ready"), sem("xn2_ready")
        xnT_psum, xnT_ready = sem("xn2_turned"), sem("xn2_T_ready")
        lg_psum, lg_read, prob_exp = sem("logits_ready"), sem("logits_read"), sem("probs_exp")
        given_ready, rank_psum, rank_read = sem("given_ready"), sem("ranks_ready"), sem("ranks_read")
        pos_ready, scattered = sem("rows_ready"), [sem("scattered0"), sem("scattered1")]
        chain_sem = sem("route_chain")
        ones_ready = sem("ones_ready")
        qk_loaded = [sem(f"qk_loaded{g}") for g in range(4)]
        shift_loaded = [sem(f"shift_loaded{g}") for g in range(4)]
        adj_loaded = [sem(f"adj_loaded{u}") for u in (0, 1)]
        v_loaded = [sem(f"v_loaded{u}") for u in (0, 1)]
        adj_ready = sem("adj_eps_added")
        st_ready, st_free = sem("scores_ready"), [sem("scores_free0"), sem("scores_free1")]
        sm_ready, max_done = sem("scores_for_max"), sem("max_done")
        exp_dve, exp_pool = sem("exp_for_dve"), sem("exp_for_pool_s")
        made_dve, made_pool = sem("products_of_dve"), sem("products_of_pool")
        pv_done, osb_ready = sem("values_summed"), sem("values_copied")
        mt_psum, mt_high, mt_rest, mt_mid, mt_low = (sem(n) for n in (
            "max_turned", "max_high", "max_rest", "max_mid", "max_low"))
        ot_psum, rec_ready, an_ready = sem("values_turned"), sem("sums_inverted"), sem("attended_ready")
        at_psum, at_ready = sem("attended_turned"), sem("attended_T_ready")
        wo_psum, x1_ready = sem("output_ready"), sem("x1_ready")

        ST = [m.psum[:, 0:2, :], m.psum[:, 2:4, :]]
        SM = m.psum[:, 4:6, :]
        OT = m.psum[:, 6, :]
        MISC = m.psum[:, 7, :]

        def every_graph(body):
            def walk(eng):
                body(-1, -1, 1, False, True, False, False)
                body(0, 0, 0, True, True, False, False)
                body(1, 0, 1, True, True, True, False)
                with eng.Fori(0, GRAPHS // 2 - 2) as i:
                    body(2 * i + 2, i + 1, 0, True, True, True, True)
                    body(2 * i + 3, i + 1, 1, True, True, True, True)
                body(GRAPHS - 2, GRAPHS // 2 - 1, 0, True, True, True, True)
                body(GRAPHS - 1, GRAPHS // 2 - 1, 1, True, False, True, True)
                body(GRAPHS, GRAPHS // 2, 0, False, False, True, True)
                body(GRAPHS + 1, GRAPHS // 2, 1, False, False, False, True)
            return walk

        with nc.Block() as block:
            @block.sync
            def _(sp):
                def load_group(b, n, u, g):
                    buf = 2 * u + g
                    wait_pos(sp, qk_loaded[buf], QK_DMAS * n)
                    cols = slice(g * GROUP * NODES, (g + 1) * GROUP * NODES)
                    for stack, first, order in ((qs, 0, Q_PARTS), (ks, 3, K_PARTS)):
                        for j, part in enumerate(order):
                            src = qk_d[b, first + part, :, :].rearrange("(d h) c -> d (h c)", d=DH)
                            sp.dma_start(stack[DH * j:DH * (j + 1), buf, :, :].rearrange("d h c -> d (h c)"),
                                         src[:, cols]).then_inc(qk_loaded[buf], 16)

                def load_adj(b, n, u):
                    sp.dma_start(adj[:, u, :, :], adj_d[b, :, :].rearrange("(t p) q -> p t q", p=P)
                                 ).then_inc(adj_loaded[u], 16)

                def load_v(b, n, u):
                    sp.dma_start(vp[:, u, :, :, :].rearrange("p t h c -> p (t h c)"), v_d[b, :, :]
                                 ).then_inc(v_loaded[u], 16)

                def load_shift(b, n, u, g):
                    y = g
                    sp.wait_ge(mt_low, 2 * b + g + 1)
                    for part in range(3):
                        sp.dma_start(qs[ROWS + part:ROWS + part + 1, 2 * u + g, :, :].rearrange(
                                         "o h (t p) -> o (h t) p", p=P),
                                     mx_parts[:, y, part, :]
                                     ).then_inc(shift_loaded[2 * u + g], 16)

                def body(b, n, u, scores, maxima, tail, ranks):
                    v, nv = 1 - u, n + u
                    if maxima:
                        wait_pos(sp, st_ready, SLOTS * b)
                        load_group(b + 1, nv, v, 1)
                        if scores:
                            wait_alone(sp, m, made_dve, N_DVE * b)
                            wait_pos(sp, made_pool, N_POOL * b)
                            load_adj(b + 1, nv, v)
                    if scores:
                        load_shift(b, n, u, 1)
                    if maxima:
                        if scores:
                            wait_pos(sp, pv_done, HALF * b)
                            load_v(b + 1, nv, v)
                        if not isinstance(b, int) or b < GRAPHS - 2:
                            if scores:
                                sp.wait_ge(st_ready, SLOTS * b + HALF)
                            load_group_next(b, n, u)
                        load_shift(b + 1, nv, v, 0)

                def load_group_next(b, n, u):
                    load_group(b + 2, n + 1, u, 0)

                load_group(0, 0, 0, 0)
                load_adj(0, 0, 0)
                load_v(0, 0, 0)
                every_graph(body)(sp)

            @block.gpsimd
            def _(pool):
                pool.memset(ks[ROWS:ROWS + 3, :, :, :], 1.0).then_inc(ones_ready, 1)
                pool.wait_ge(ones_ready, 1)

                pool.memset(minus_half[:, :], -0.5).then_inc(ones_ready, 1)
                pool.wait_ge(ones_ready, 2)

                def product(b, n, u, s):
                    k, kt = POOL_SLOTS.index(s), s % HALF // 2
                    pool.wait_ge(exp_pool, N_POOL * b + k + 1)
                    wait_pos(pool, pv_done, HALF * b + (s - 4) // 2 + 1)
                    e = (N_POOL * u + k) % 2
                    pool.tensor_tensor(pr[:, s % 4, :, :], ex[:, e, :, :],
                                       adj[:, u, kt, :].unsqueeze(1).to_broadcast([P, 2, NODES]),
                                       ALU.mult).then_inc(made_pool, 1)

                def scatter(c, cu, t):
                    if t == 0:
                        wait_alone(pool, m, pos_ready, c + 1)
                    for k in range(TOP):
                        pool.indirect_dma_start(
                            rows_d[:, :], bass.IndirectOffsetOnAxis(ap=pos2[:, cu, t, k:k + 1], axis=0),
                            xn[:, cu, t, :], None).then_inc(scattered[cu], 16)

                def body(b, n, u, scores, maxima, tail, ranks):
                    if scores:
                        wait_alone(pool, m, adj_loaded[u], 16 * n + 16)
                        pool.tensor_scalar(adj[:, u, :, :], adj[:, u, :, :], ADJ_EPS, 1.0,
                                           ALU.add, ALU.mult).then_inc(adj_ready, 1)
                        pool.wait_ge(adj_ready, b + 1)
                    for s in range(SLOTS):
                        if scores and s in POOL_SLOTS:
                            product(b, n, u, s)
                        if ranks and s in (2, 5, 8, 11):
                            scatter(b - 2, u, (s - 2) // 3)
                        if s == 9 and tail:
                            pool.wait_ge(var_ready, b)
                            pool.tensor_tensor(rstd[:, :], var_eps[:, :], minus_half[:, :],
                                               ALU.pow).then_inc(rstd_ready, 1)
                every_graph(body)(pool)
                for u in (0, 1):
                    pool.wait_ge(scattered[u], 16 * TILES * TOP * GRAPHS // 2)

            @block.scalar
            def _(act):
                def values_copy(b, g):
                    act.wait_ge(pv_done, HALF * b + 4 * g + 4)
                    wait_pos(act, ot_psum, 2 * b + g)
                    act.copy(osb[:, :], OT).then_inc(osb_ready, 1)

                def max_high(b, g):
                    y = g
                    act.wait_ge(mt_psum, 2 * b + g + 1)
                    act.copy(mx_parts[:, y, 0, :], MISC[0:16, 0:P]).then_inc(mt_high, 1)

                def body(b, n, u, scores, maxima, tail, ranks):
                    for s in range(SLOTS):
                        kt, pair, g = s % HALF // 2, s % 2, s // HALF
                        if scores:
                            act.wait_ge(st_ready, SLOTS * b + s + 1)
                            if s in POOL_SLOTS:
                                k = POOL_SLOTS.index(s)
                                e = (N_POOL * u + k) % 2
                                wait_pos(act, made_pool, N_POOL * b + k - 1)
                                act.activation(ex[:, e, :, :], ST[s % 2], ACT.Exp, scale=DH ** -0.5
                                               ).then_inc(exp_pool, 1)
                                act.wait_ge(exp_pool, N_POOL * b + k + 1)
                                act.sem_inc(st_free[s % 2], 1)
                            else:
                                act.activation(ST[s % 2], ST[s % 2], ACT.Exp, scale=DH ** -0.5
                                               ).then_inc(exp_dve, 1)
                        if s == 0 and scores:
                            max_high(b, 1)
                        if s == 1 and tail:
                            values_copy(b - 1, 1)
                        if s == 5 and tail:
                            act.wait_ge(at_psum, b)
                            wait_pos(act, wo_psum, b - 1)
                            act.copy(anT[:, :], MISC).then_inc(at_ready, 1)
                        if s == 8 and maxima:
                            max_high(b + 1, 0)
                        if s == 9 and scores:
                            values_copy(b, 0)
                        if s == 12 and tail:
                            act.wait_ge(xnT_psum, b)
                            act.copy(xnT[:, :], MISC).then_inc(xnT_ready, 1)
                        if s == 14 and tail:
                            act.wait_ge(lg_read, b)
                            act.activation(prob[:, :, :], prob[:, :, :], ACT.Exp).then_inc(prob_exp, 1)
                every_graph(body)(act)

            @block.vector
            def _(dve):
                dve.sem_inc(st_free[0], 1)
                dve.sem_inc(st_free[1], 1)
                for u in (0, 1):
                    dve.tensor_scalar_add(xn[:, u, :, TOKEN], m.small[:, 2 * EXPERTS:],
                                          float((u - 2) * NODES))

                def max_low(b, g):
                    i, y = 2 * b + g, g
                    dve.wait_ge(mt_high, i + 1)
                    dve.tensor_tensor(mx_rest[:, y, :], MISC[0:16, 0:P], mx_parts[:, y, 0, :],
                                      ALU.subtract).then_inc(mt_rest, 1)
                    dve.wait_ge(mt_rest, i + 1)
                    dve.tensor_copy(mx_parts[:, y, 1, :], mx_rest[:, y, :]).then_inc(mt_mid, 1)
                    dve.wait_ge(mt_mid, i + 1)
                    dve.tensor_tensor(mx_parts[:, y, 2, :], mx_rest[:, y, :], mx_parts[:, y, 1, :],
                                      ALU.subtract).then_inc(mt_low, 1)

                def normalise(b, g):
                    i = 2 * b + g
                    t = MISC.rearrange("p (t j c) -> p t j c", t=TILES, c=32)
                    dve.wait_ge(ot_psum, i + 1)
                    dve.reciprocal(rec[:, :, :], t[:, :, :, DH]).then_inc(rec_ready, 1)
                    dve.wait_ge(rec_ready, i + 1)
                    if g == 0:
                        wait_pos(dve, at_psum, b)
                    out = an[:, :, g * 64:g * 64 + 64].rearrange("p t (j d) -> p t j d", d=DH)
                    dve.tensor_tensor(out, t[:, :, :, 0:DH],
                                      rec[:, :, :].unsqueeze(3).to_broadcast([P, TILES, GROUP, DH]),
                                      ALU.mult).then_inc(an_ready, 1)

                LINKS, AT_ROUTE, AT_PICK = 20, 2, 18

                def norm_stats(c):
                    ch = Chain(dve, chain_sem, LINKS * c)
                    for t in range(TILES):
                        last = dve.bn_stats(stats[:, t, :], m.x[:, c * TILES + t, :])
                    ch.link(last, m)
                    for t in range(TILES):
                        last = dve.bn_aggr(mv[:, t, :], stats[:, t, :])
                    ch.link(last)
                    dve.tensor_scalar_add(var_eps[:, :], mv[:, :, 1], LN_EPS).then_inc(var_ready, 1)

                def norm(c, cn, cu):
                    dve.wait_ge(rstd_ready, c + 1)
                    wait_pos(dve, scattered[cu], 16 * TILES * TOP * cn)
                    for t in range(TILES):
                        dve.tensor_scalar(xn[:, cu, t, 0:HID], m.x[:, c * TILES + t, :],
                                          mv[:, t, 0:1], rstd[:, t:t + 1], ALU.subtract, ALU.mult)
                    dve.tensor_scalar_add(xn[:, cu, :, TOKEN], xn[:, cu, :, TOKEN], 2.0 * NODES
                                          ).then_inc(xn_ready, 1)

                def logits_shift(c):
                    ch = Chain(dve, chain_sem, LINKS * c + AT_ROUTE)
                    lg = MISC[:, 0:TILES * EXPERTS].rearrange("p (t e) -> p t e", e=EXPERTS)
                    dve.wait_ge(lg_psum, c + 1)
                    ch.link(dve.tensor_reduce(lmax[:, :], lg, AX.X, ALU.max, negate=True))
                    dve.tensor_tensor(prob[:, :, :], lg,
                                      lmax[:, :].unsqueeze(2).to_broadcast([P, TILES, EXPERTS]),
                                      ALU.add).then_inc(lg_read, 1)

                def choose(c, cu):
                    ch = Chain(dve, chain_sem, LINKS * c + AT_ROUTE + 1)
                    dve.wait_ge(prob_exp, c + 1)
                    ch.link(dve.tensor_reduce(psum_inv[:, 0, :], prob[:, :, :], AX.X, ALU.add))
                    ch.link(dve.reciprocal(psum_inv[:, 1, :], psum_inv[:, 0, :]))
                    ch.link(dve.tensor_tensor(
                        prob[:, :, :], prob[:, :, :],
                        psum_inv[:, 1, :].unsqueeze(2).to_broadcast([P, TILES, EXPERTS]), ALU.mult), m)
                    for t in range(TILES):
                        last = dve.max(top[:, t, :], prob[:, t, :])
                    ch.link(last, m)
                    for t in range(TILES):
                        last = dve.max_index(topi[:, t, :], top[:, t, :], prob[:, t, :])
                    ch.link(last)
                    dve.tensor_copy(topf[:, :, :], topi[:, :, 0:TOP])
                    dve.tensor_copy(xn[:, cu, :, FIRST], topi[:, :, 0])
                    ch.link(dve.tensor_tensor(tsum[:, 0, :], top[:, :, 0], top[:, :, 1], ALU.add))
                    ch.link(dve.tensor_scalar_add(tsum[:, 0, :], tsum[:, 0, :], 1e-9))
                    ch.link(dve.reciprocal(tsum[:, 1, :], tsum[:, 0, :]))
                    dve.tensor_tensor(m.gates[:, bass.ds(c * TILES, TILES), :], top[:, :, 0:TOP],
                                      tsum[:, 1, :].unsqueeze(2).to_broadcast([P, TILES, TOP]), ALU.mult)
                    ch.link(dve.tensor_tensor(
                        hot[:, :, :, :].rearrange("p t k e -> p (t k) e"),
                        m.small[:, 0:EXPERTS].unsqueeze(1).to_broadcast([P, TILES * TOP, EXPERTS]),
                        topf[:, :, :].rearrange("p t k -> p (t k)").unsqueeze(2).to_broadcast(
                            [P, TILES * TOP, EXPERTS]), ALU.is_equal))
                    ch.link(dve.tensor_copy(m.counts[:, 0, :], m.counts[:, TILES, :]))
                    ch.link(dve.tensor_tensor(given[:, :, :], hot[:, :, 0, :], hot[:, :, 1, :], ALU.add))
                    for t in range(TILES):
                        last = dve.tensor_tensor(m.counts[:, t + 1, :], m.counts[:, t, :], given[:, t, :],
                                                 ALU.add)
                        ch.link(last)
                    assert AT_ROUTE + 1 + ch.n == AT_PICK
                    dve.sem_inc(given_ready, 1)

                def pick_rows(c, cu):
                    ch = Chain(dve, chain_sem, LINKS * c + AT_PICK)
                    dve.wait_ge(rank_psum, c + 1)
                    rk = MISC[:, 0:TILES * EXPERTS].rearrange("p (t e) -> p t e", e=EXPERTS)
                    dve.tensor_tensor(rank[:, :, :], rk, m.small[:, EXPERTS:2 * EXPERTS].unsqueeze(1)
                                      .to_broadcast([P, TILES, EXPERTS]), ALU.add).then_inc(rank_read, 1)
                    dve.wait_ge(rank_read, c + 1)
                    ch.link(dve.tensor_tensor(
                        picked[:, :, :, :], hot[:, :, :, :],
                        rank[:, :, :].unsqueeze(2).to_broadcast([P, TILES, TOP, EXPERTS]), ALU.mult))
                    ch.link(dve.tensor_reduce(posf[:, :, :], picked[:, :, :, :], AX.X, ALU.add))
                    assert AT_PICK + ch.n == LINKS
                    dve.tensor_copy(pos2[:, cu, :, :], posf[:, :, :]).then_inc(pos_ready, 1)

                def body(b, n, u, scores, maxima, tail, ranks):
                    for s in range(SLOTS):
                        kt, pair, g = s % HALF // 2, s % 2, s // HALF
                        if maxima:
                            i = SLOTS * (b + 1) + s
                            col = (s % HALF // 2) * TILES + 2 * (s % 2)
                            dve.wait_ge(sm_ready, i + 1)
                            dve.tensor_reduce(mx[:, 2 * (1 - u) + g, col:col + 2], SM, AX.X, ALU.max,
                                              negate=True).then_inc(max_done, 1)
                        if scores and s not in POOL_SLOTS:
                            k = dve_made(s) - 1
                            if k == 0:
                                dve.wait_ge(adj_ready, b + 1)
                            dve.wait_ge(exp_dve, N_DVE * b + k + 1)
                            wait_pos(dve, pv_done, HALF * b + (s - 4) // 2 + 1)
                            dve.tensor_tensor(pr[:, s % 4, :, :], ST[s % 2],
                                              adj[:, u, kt, :].unsqueeze(1).to_broadcast([P, 2, NODES]),
                                              ALU.mult).then_inc(made_dve, 1)
                            dve.wait_ge(made_dve, N_DVE * b + k + 1)
                            dve.sem_inc(st_free[s % 2], 1)
                        if s == 0 and scores:
                            max_low(b, 1)
                        if s == 3 and tail:
                            normalise(b - 1, 1)
                        if s == 7 and tail:
                            xb = m.x[:, bass.ds((b - 1) * TILES, TILES), :]
                            dve.wait_ge(wo_psum, b)
                            dve.tensor_tensor(xb, MISC.rearrange("p (t c) -> p t c", t=TILES), xb,
                                              ALU.add).then_inc(x1_ready, 1)
                        if s == 8 and maxima:
                            max_low(b + 1, 0)
                        if s == 11 and scores:
                            normalise(b, 0)
                        if s == 1 and ranks:
                            pick_rows(b - 2, u)
                        if s == 8 and tail:
                            wait_alone(dve, m, x1_ready, b)
                            norm_stats(b - 1)
                        if s == 10 and tail:
                            norm(b - 1, n - (1 - u), 1 - u)
                        if s == 14 and tail:
                            logits_shift(b - 1)
                        if s == 15 and tail:
                            choose(b - 1, 1 - u)
                every_graph(body)(dve)
                dve.wait_ge(pos_ready, GRAPHS)

            @block.tensor
            def _(pe):
                pe.wait_ge(ones_ready, 1)

                def body(b, n, u, scores, maxima, tail, ranks):
                    v, nv = 1 - u, n + u
                    for s in range(SLOTS):
                        kt, pair, g = s % HALF // 2, s % 2, s // HALF
                        if scores:
                            buf = 2 * u + g
                            if s % HALF == 0:
                                pe.wait_ge(shift_loaded[buf], 48 * n + 48)
                            pe.wait_ge(st_free[s % 2], HALF * b + s // 2 + 1)
                            for h in (0, 1):
                                hl = 2 * pair + h
                                last = pe.matmul(ST[s % 2][:, h, :],
                                                 ks[0:ROWS + 3, buf, hl, kt * P:(kt + 1) * P],
                                                 qs[0:ROWS + 3, buf, hl, :], start=True, stop=True)
                            last.then_inc(st_ready, 1)
                        if maxima:
                            buf = 2 * v + g
                            i = SLOTS * (b + 1) + s
                            hl, q0 = s % HALF // 2, 2 * (s % 2)
                            if s % HALF == 0:
                                pe.wait_ge(qk_loaded[buf], QK_DMAS * nv + QK_DMAS)
                            wait_pos(pe, max_done, i)
                            for q in (0, 1):
                                last = pe.matmul(SM[:, q, :],
                                                 qs[0:ROWS, buf, hl, (q0 + q) * P:(q0 + q + 1) * P],
                                                 ks[0:ROWS, buf, hl, :], start=True, stop=True)
                            last.then_inc(sm_ready, 1)

                        if s % 2 and (scores if s >= 3 else tail):
                            if s >= 3:
                                vb, vu, vn, t, gg = b, u, n, (s - 3) % HALF // 2, (s - 3) // HALF
                                dve_n = N_DVE * b + dve_made(s - 2)
                                pool_n = N_POOL * b + pool_made(s - 2)
                            else:
                                vb, vu, vn, t, gg = b - 1, 1 - u, n - (1 - u), TILES - 1, 1
                                dve_n, pool_n = N_DVE * b, N_POOL * b
                            if t == 0:
                                wait_pos(pe, osb_ready, 2 * vb + gg)
                                if gg == 0:
                                    pe.wait_ge(v_loaded[vu], 16 * vn + 16)
                            wait_pos(pe, made_dve, dve_n)
                            wait_pos(pe, made_pool, pool_n)
                            for j in range(GROUP):
                                slot = (s - 3 + j // 2) % 4
                                last = pe.matmul(OT[32 * j:32 * j + 32, :],
                                                 vp[:, vu, t, gg * GROUP + j, :], pr[:, slot, j % 2, :],
                                                 start=(t == 0), stop=(t == TILES - 1),
                                                 skip_group_check=True)
                            last.then_inc(pv_done, 1)

                        def turn_max(bb, gg, buf):
                            pe.wait_ge(max_done, SLOTS * bb + HALF * gg + HALF)
                            pe.transpose(MISC[0:16, 0:P], mx[:, buf, :], m.ident[:, :]).then_inc(mt_psum, 1)

                        def turn_values(bb, gg):
                            pe.wait_ge(osb_ready, 2 * bb + gg + 1)
                            for t in range(TILES):
                                last = pe.transpose(MISC[:, t * P:(t + 1) * P], osb[:, t * P:(t + 1) * P],
                                                    m.ident[:, :])
                            last.then_inc(ot_psum, 1)

                        if s == 0 and scores:
                            if tail:
                                wait_pos(pe, an_ready, 2 * b - 1)
                                wait_pos(pe, lg_read, b - 1)
                            turn_max(b, 1, 2 * u + 1)
                        if s == 1 and ranks:
                            if scores:
                                pe.wait_ge(mt_rest, 2 * b + 2)
                            pe.wait_ge(given_ready, b - 1)
                            rk = MISC[:, 0:TILES * EXPERTS]
                            pe.matmul(rk, m.before[:, :], given[:, :, :].rearrange("p t e -> p (t e)"),
                                      start=True, stop=False)
                            pe.matmul(rk, m.ones[:, :],
                                      m.counts[:, 0:TILES, :].rearrange("p t e -> p (t e)"),
                                      start=False, stop=True).then_inc(rank_psum, 1)
                        if s == 2 and tail:
                            if scores:
                                pe.wait_ge(mt_rest, 2 * b + 2)
                            if ranks:
                                pe.wait_ge(rank_read, b - 1)
                            turn_values(b - 1, 1)
                        if s == 4 and tail:
                            pe.wait_ge(an_ready, 2 * b)
                            for t in range(TILES):
                                last = pe.transpose(MISC[:, t * P:(t + 1) * P], an[:, t, :], m.ident[:, :])
                            last.then_inc(at_psum, 1)
                        if s == 6 and tail:
                            pe.wait_ge(at_ready, b)
                            for t in range(TILES):
                                last = pe.matmul(MISC[:, t * P:(t + 1) * P], anT[:, t * P:(t + 1) * P],
                                                 m.wo[:, :], start=True, stop=True)
                            last.then_inc(wo_psum, 1)
                        if s == 8 and maxima:
                            wait_pos(pe, x1_ready, b)
                            turn_max(b + 1, 0, 2 * v)
                        if s == 10 and scores:
                            if maxima:
                                pe.wait_ge(mt_rest, 2 * b + 3)
                            else:
                                pe.wait_ge(x1_ready, b)
                            turn_values(b, 0)
                        if s == 12 and tail:
                            if scores:
                                pe.wait_ge(an_ready, 2 * b + 1)
                            pe.wait_ge(xn_ready, b)
                            wait_pos(pe, x1_ready, b)
                            for t in range(TILES):
                                last = pe.transpose(MISC[:, t * P:(t + 1) * P], xn[:, 1 - u, t, 0:HID],
                                                    m.ident[:, :])
                            last.then_inc(xnT_psum, 1)
                        if s == 13 and tail:
                            pe.wait_ge(xnT_ready, b)
                            for t in range(TILES):
                                last = pe.matmul(MISC[:, t * EXPERTS:(t + 1) * EXPERTS],
                                                 xnT[:, t * P:(t + 1) * P], m.router[:, :],
                                                 start=True, stop=True)
                            last.then_inc(lg_psum, 1)
                every_graph(body)(pe)


def stage_experts(nc, m, w13_d, w2_d, rows_d, outs_d):
    I32, U32 = mybir.dt.int32, mybir.dt.uint32
    SHIFT = BLOCK.bit_length() - 1
    with ExitStack() as ctx:
        def sb(name, shape, dt=F32):
            return ctx.enter_context(nc.sbuf_tensor(name, shape, dt))

        def sem(name):
            return ctx.enter_context(nc.semaphore(name))

        E, NB = EXPERTS, N_BLOCKS
        empty = sb("empty_rows", [P, SUB, WIDE])
        count = sb("expert_count", [P, E])
        full = sb("expert_blocks_int", [P, 2, E], I32)
        many = sb("expert_blocks", [P, E])
        none = sb("no_blocks", [P, E])
        last_b = sb("blocks_up_to", [P, E])
        first_b = sb("first_block", [P, E])
        past = sb("past_expert", [P, NB, E])
        begun = sb("begun_expert", [1, NB, E])
        where = sb("row_if_expert", [1, NB, E])
        number = sb("expert_of_block_f", [P, NB])
        spill = sb("is_trash", [1, NB])
        src_f, end_f = sb("read_row_f", [1, NB]), sb("end_row_f", [1, E])
        exp_i, src_i, end_i = (sb(n, [1, NB], U32) for n in ("expert_of_block", "read_row", "end_row"))
        xr = sb("block_rows", [P, DEEP, SUB, WIDE])
        xT = sb("block_T", [P, 2, BLOCK])
        w13 = sb("w13_block", [P, DEEP, 2, FT, P])
        w2 = sb("w2_block", [P, DEEP, FT, HID])
        act1 = sb("silu_h1", [P, 2, FT, BLOCK])
        hid = sb("hidden", [P, 2, FT, BLOCK])
        yr = sb("block_out", [P, DEEP, SUB, HID])
        second = sb("offset_if_second", [P, DEEP, SUB])
        dest = sb("row_of_result", [P, DEEP, SUB], U32)

        e_ready, cnt_psum, tab_chain, tab_ready = (sem(n) for n in (
            "empty_rows_ready", "counts_summed", "table_chain", "table_ready"))
        ends = sem("region_ends_emptied")
        loaded = [sem(f"block_loaded{q}") for q in range(DEEP)]
        xT_psum, xT_ready, h_psum, act_ready, hid_ready, y_psum, y_ready = (sem(n) for n in (
            "block_turned", "block_T_ready", "h_ready", "silu_ready", "hidden_ready", "y_summed", "y_ready"))
        off_ready, dest_ready = sem("offset_ready"), sem("dest_ready")
        y_out = [sem(f"block_stored{q}") for q in range(DEEP)]

        H = [m.psum[:, 0:FT, :], m.psum[:, FT:2 * FT, :]]
        XT, Y = m.psum[:, 6, :], m.psum[:, 7, :]

        def every_block(step):
            def walk(eng):
                with eng.Fori(0, NB // DEEP) as i:
                    for q in range(DEEP):
                        step(DEEP * i + q, i, q)
            return walk

        def staggered(step):
            def walk(eng):
                step(0, 0, 0)
                with eng.Fori(0, NB // DEEP - 1) as i:
                    for c in range(1, DEEP + 1):
                        step(DEEP * i + c, i + c // DEEP, c % DEEP)
                for j in range(NB - DEEP + 1, NB + 1):
                    step(j, j // DEEP, j % DEEP)
            return walk

        def is_int(j, *values):
            return isinstance(j, int) and j in values

        with nc.Block() as block:
            @block.gpsimd
            def _(pool):
                pool.memset(empty[:, :, 0:FIRST], 0.0)
                pool.memset(empty[:, :, FIRST:TOKEN], -1.0)
                for t in range(SUB):
                    last = pool.memset(empty[:, t, TOKEN:WIDE], float(TOKENS + t))
                last.then_inc(e_ready, 1)

                def step(j, r, q):
                    wait_alone(pool, m, y_out[(q - 1) % DEEP], 16 * SUB * (r + 1 if q else r))
                    wait_alone(pool, m, y_ready, j + 1 + 1)
                    wait_alone(pool, m, dest_ready, j + 1 + DEEP)
                    for t in range(SUB):
                        pool.indirect_dma_start(
                            outs_d[:, :], bass.IndirectOffsetOnAxis(ap=dest[:, q, t:t + 1], axis=0),
                            yr[:, q, t, :], None).then_inc(y_out[q], 16)
                every_block(step)(pool)
                for q in range(DEEP):
                    pool.wait_ge(y_out[q], 16 * SUB * (NB // DEEP))

            @block.vector
            def _(dve):
                ch = Chain(dve, tab_chain, 0)
                L = ch.link
                dve.wait_ge(cnt_psum, 1)
                L(dve.tensor_copy(count[:, :], m.psum[:, 7, 0:E]))
                L(dve.tensor_scalar_add(full[:, 0, :], count[:, :], float(BLOCK - 1)))
                L(dve.tensor_single_scalar(full[:, 1, :], full[:, 0, :], SHIFT, ALU.arith_shift_right))
                L(dve.tensor_copy(many[:, :], full[:, 1, :]))
                L(dve.memset(none[:, :], 0.0))
                L(dve.tensor_tensor_scan(last_b[:, :], many[:, :], none[:, :], 0.0, ALU.add, ALU.add))
                L(dve.tensor_tensor(first_b[:, :], last_b[:, :], many[:, :], ALU.subtract))
                L(dve.tensor_tensor(end_f[:, :], m.small[0:1, E:2 * E], count[0:1, :], ALU.add))
                L(dve.tensor_copy(end_i[:, 0:E], end_f[:, :]))
                nb = m.blocks[0:1, :].unsqueeze(2).to_broadcast([1, NB, E])

                def per_expert(a):
                    return a.unsqueeze(1).to_broadcast([1, NB, E])
                L(dve.tensor_tensor(past[:, :, :], m.blocks[:, :].unsqueeze(2).to_broadcast([P, NB, E]),
                                    last_b[:, :].unsqueeze(1).to_broadcast([P, NB, E]), ALU.is_ge))
                L(dve.tensor_tensor(begun[:, :, :], nb, per_expert(first_b[0:1, :]), ALU.is_ge))
                L(dve.tensor_tensor(begun[:, :, :], begun[:, :, :], past[0:1, :, :], ALU.subtract))
                L(dve.tensor_reduce(number[:, :], past[:, :, :], AX.X, ALU.add))
                L(dve.tensor_tensor(where[:, :, :], nb, per_expert(first_b[0:1, :]), ALU.subtract))
                L(dve.tensor_scalar(where[:, :, :], where[:, :, :], float(BLOCK), None, ALU.mult))
                L(dve.tensor_tensor(where[:, :, :], where[:, :, :], per_expert(m.small[0:1, E:2 * E]), ALU.add))
                L(dve.tensor_tensor(where[:, :, :], where[:, :, :], begun[:, :, :], ALU.mult))
                L(dve.tensor_reduce(src_f[:, :], where[:, :, :], AX.X, ALU.add))
                L(dve.tensor_scalar(spill[:, :], number[0:1, :], float(E), float(TRASH), ALU.is_ge, ALU.mult))
                L(dve.tensor_tensor(src_f[:, :], src_f[:, :], spill[:, :], ALU.add))
                L(dve.tensor_scalar(number[:, :], number[:, :], float(E - 1), None, ALU.min))
                L(dve.tensor_copy(exp_i[:, :], number[0:1, :]))
                dve.tensor_copy(src_i[:, :], src_f[:, :]).then_inc(tab_ready, 1)

                dve.sem_inc(hid_ready, 2)
                dve.sem_inc(act_ready, 2)
                dve.sem_inc(dest_ready, DEEP)

                def step(j, r, q):
                    dve.wait_ge(loaded[q], 48 * r + 48)
                    dve.wait_ge(y_out[q], 16 * SUB * r)
                    dve.tensor_scalar(second[:, q, :], xr[:, q, :, FIRST], number[:, bass.ds(j, 1)],
                                      float(TOKENS), ALU.not_equal, ALU.mult).then_inc(off_ready, 1)
                    dve.wait_ge(off_ready, j + 1)
                    dve.tensor_tensor(dest[:, q, :], second[:, q, :], xr[:, q, :, TOKEN],
                                      ALU.add).then_inc(dest_ready, 1)
                    dve.wait_ge(act_ready, j + 1 + 2)
                    dve.wait_ge(y_psum, j - 1 + DEEP)
                    dve.tensor_tensor(hid[:, q % 2, :, :], act1[:, q % 2, :, :],
                                      H[q % 2][:, :, BLOCK:2 * BLOCK], ALU.mult).then_inc(hid_ready, 1)
                every_block(step)(dve)

            @block.sync
            def _(sp):
                sp.wait_ge(e_ready, 1)
                sp.wait_ge(tab_ready, 1)

                def empty_rows(row):
                    sp.dma_start(rows_d[bass.ds(row, BLOCK), :].rearrange("(p s) c -> p s c", s=SUB),
                                 empty[:, :, :]).then_inc(ends, 16)
                for e in range(E):
                    r = sp.value_load(end_i[0:1, e:e + 1], min_val=0, max_val=TRASH - BLOCK)
                    empty_rows(r)
                empty_rows(TRASH)
                sp.wait_ge(ends, 16 * (E + 1))

                def step(j, r, q):
                    sp.wait_ge(y_psum, j + 1)
                    sp.wait_ge(dest_ready, j + 1)
                    row = sp.value_load(src_i[0:1, bass.ds(j, 1)], min_val=0, max_val=TRASH)
                    e = sp.value_load(exp_i[0:1, bass.ds(j, 1)], min_val=0, max_val=E - 1)
                    sp.dma_start(xr[:, q, :, :], rows_d[bass.ds(row, BLOCK), :].rearrange(
                        "(p s) c -> p s c", s=SUB)).then_inc(loaded[q], 16)
                    sp.dma_start(w13[:, q, :, :, :].rearrange("p a t h -> p (a t h)"),
                                 w13_d[bass.ds(e, 1), :, :].squeeze(0)).then_inc(loaded[q], 16)
                    sp.dma_start(w2[:, q, :, :].rearrange("p t c -> p (t c)"),
                                 w2_d[bass.ds(e, 1), :, :].squeeze(0)).then_inc(loaded[q], 16)
                every_block(step)(sp)

            @block.tensor
            def _(pe):
                pe.matmul(m.psum[:, 7, 0:E], m.ones[:, :], m.counts[:, TILES, :],
                          start=True, stop=True).then_inc(cnt_psum, 1)
                pe.wait_ge(tab_ready, 1)
                pe.sem_inc(y_psum, DEEP)

                def turn(j, r, q):
                    pe.wait_ge(loaded[q], 48 * r + 48)
                    for t in range(SUB):
                        last = pe.transpose(XT[:, t * P:(t + 1) * P], xr[:, q, t, 0:HID], m.ident[:, :])
                    last.then_inc(xT_psum, 1)

                def step(j, r, q):
                    if not is_int(j, NB):
                        pe.wait_ge(xT_ready, j + 1)
                        pe.wait_ge(hid_ready, j + 1)
                        for t in range(FT):
                            for a in (0, 1):
                                last = pe.matmul(H[q % 2][:, t, a * BLOCK:(a + 1) * BLOCK],
                                                 w13[:, q, a, t, :], xT[:, q % 2, :],
                                                 start=True, stop=True)
                        last.then_inc(h_psum, 1)
                    if not is_int(j, NB - 1, NB):
                        turn(j + 1, r + (q + 1) // DEEP, (q + 1) % DEEP)
                    if not is_int(j, 0):
                        pe.wait_ge(hid_ready, j + 2)
                        pe.wait_ge(y_ready, j)
                        for t2 in range(SUB):
                            for t in range(FT):
                                last = pe.matmul(Y[:, t2 * P:(t2 + 1) * P],
                                                 hid[:, (q - 1) % 2, t, t2 * P:(t2 + 1) * P],
                                                 w2[:, (q - 1) % DEEP, t, :],
                                                 start=(t == 0), stop=(t == FT - 1))
                        last.then_inc(y_psum, 1)
                turn(0, 0, 0)
                staggered(step)(pe)

            @block.scalar
            def _(act):
                act.sem_inc(y_ready, 1)

                def turned(j, q):
                    act.wait_ge(xT_psum, j + 1)
                    act.copy(xT[:, q % 2, :], XT[:, 0:BLOCK]).then_inc(xT_ready, 1)

                def step(j, r, q):
                    if not is_int(j, NB):
                        act.wait_ge(h_psum, j + 1)
                        act.wait_ge(hid_ready, j + 1)
                        act.activation(act1[:, q % 2, :, :], H[q % 2][:, :, 0:BLOCK], ACT.Silu
                                       ).then_inc(act_ready, 1)
                    if not is_int(j, NB - 1, NB):
                        turned(j + 1, q + 1)
                    if not is_int(j, 0):
                        act.wait_ge(y_psum, j + DEEP)
                        wait_pos(act, y_out[(q - 1) % DEEP], 16 * SUB * (r if q else r - 1))
                        act.copy(yr[:, (q - 1) % DEEP, :, :],
                                 Y[:, 0:SUB * HID].rearrange("p (s c) -> p s c", s=SUB)
                                 ).then_inc(y_ready, 1)
                turned(0, 0)
                staggered(step)(act)


def stage_combine(nc, m, outs_d, out_d):
    with ExitStack() as ctx:
        def sb(name, shape, dt=F32):
            return ctx.enter_context(nc.sbuf_tensor(name, shape, dt))

        def sem(name):
            return ctx.enter_context(nc.semaphore(name))

        got = sb("results_of_choices", [P, DEEP, TOP, TILES, HID])
        res = sb("result", [P, DEEP, TILES, HID])
        loaded = [sem(f"results_loaded{q}") for q in range(DEEP)]
        stored = [sem(f"stored{q}") for q in range(DEEP)]
        first_added, res_ready = sem("first_added"), sem("result_ready")

        def every_graph(step):
            def walk(eng):
                with eng.Fori(0, GRAPHS // DEEP) as i:
                    for q in range(DEEP):
                        step(DEEP * i + q, i, q)
            return walk

        with nc.Block() as block:
            @block.sync
            def _(sp):
                def step(b, r, q):
                    sp.wait_ge(res_ready, b + 1)
                    for k in range(TOP):
                        sp.dma_start(got[:, q, k, :, :],
                                     outs_d[bass.ds(b * NODES + k * TOKENS, NODES), :].rearrange(
                                         "(t p) c -> p t c", p=P)).then_inc(loaded[q], 16)
                every_graph(step)(sp)

            @block.vector
            def _(dve):
                dve.sem_inc(res_ready, DEEP)

                def step(b, r, q):
                    dve.wait_ge(loaded[q], 32 * r + 32)
                    dve.wait_ge(stored[q], 16 * r + 16)
                    for t in range(TILES):
                        last = dve.scalar_tensor_tensor(res[:, q, t, :], got[:, q, 0, t, :],
                                                        m.gates[:, b * TILES + t, 0:1],
                                                        m.x[:, b * TILES + t, :], ALU.mult, ALU.add)
                    last.then_inc(first_added, 1)
                    dve.wait_ge(first_added, b + 1)
                    for t in range(TILES):
                        last = dve.scalar_tensor_tensor(res[:, q, t, :], got[:, q, 1, t, :],
                                                        m.gates[:, b * TILES + t, 1:2],
                                                        res[:, q, t, :], ALU.mult, ALU.add)
                    last.then_inc(res_ready, 1)
                every_graph(step)(dve)

            @block.scalar
            def _(act):
                for q in range(DEEP):
                    act.sem_inc(stored[q], 16)

                def step(b, r, q):
                    act.wait_ge(res_ready, b + 1 + DEEP)
                    act.dma_start(out_d[b, :, :].rearrange("(t p) c -> p t c", p=P), res[:, q, :, :]
                                  ).then_inc(stored[q], 16)
                every_graph(step)(act)
                for q in range(DEEP):
                    act.wait_ge(stored[q], 16 + 16 * (GRAPHS // DEEP))


def build(nc, x, adjT, wq, wk, wv, wo, bo, router, before, small, blocks, w13, w2, out):
    with ExitStack() as ctx:
        m = place(nc, ctx)
        qk = nc.dram_tensor("qk_parts_dram", [GRAPHS, 6, P, NODES], BF16).ap()
        v = nc.dram_tensor("v_padded_dram", [GRAPHS, P, TILES * HEADS * 32], F32).ap()
        rows = nc.dram_tensor("rows_by_expert", [TRASH + BLOCK, WIDE], F32).ap()
        outs = nc.dram_tensor("outs_by_choice", [TOP * TOKENS + SUB, HID], F32).ap()
        stage_projections(nc, m, x, (wq, wk, wv, wo, bo, router, before, small, blocks), qk, v)
        stage_attention(nc, m, adjT, qk, v, rows)
        stage_experts(nc, m, w13, w2, rows, outs)
        stage_combine(nc, m, outs, out)


def layout(x, adj, Wq, Wk, Wv, Wo, bo, router_w, w1, w2, w3):
    import numpy as np

    c = np.ascontiguousarray
    by_place = np.arange(HID).reshape(HEADS, DH).T.reshape(-1)
    w13 = np.zeros((EXPERTS, HID, 2, FT * P), np.float32)
    w13[:, :, 0, :FFN] = w1.transpose(0, 2, 1)
    w13[:, :, 1, :FFN] = w3.transpose(0, 2, 1)
    w2p = np.zeros((EXPERTS, FT * P, HID), np.float32)
    w2p[:, :FFN, :] = w2.transpose(0, 2, 1)
    small = np.zeros((P, 2 * EXPERTS + TILES), np.float32)
    small[:, :EXPERTS] = np.arange(EXPERTS)
    small[:, EXPERTS:2 * EXPERTS] = np.arange(EXPERTS) * REGION
    small[:, 2 * EXPERTS:] = np.arange(NODES).reshape(TILES, P).T
    return {
        "x": c(x), "adjT": c(adj.transpose(0, 2, 1)),
        "wq": c(Wq[by_place].T), "wk": c(Wk[by_place].T), "wv": c(Wv.T), "wo": c(Wo.T),
        "bo": c(np.broadcast_to(bo, (P, HID))), "router": c(router_w.T),
        "before": np.triu(np.ones((P, P), np.float32), 1),
        "small": small,
        "blocks": c(np.broadcast_to(np.arange(N_BLOCKS, dtype=np.float32), (P, N_BLOCKS))),
        "w13": w13.reshape(EXPERTS, HID, 2 * FT * P),
        "w2": c(w2p.reshape(EXPERTS, FT, P, HID).transpose(0, 2, 1, 3)).reshape(EXPERTS, P, FT * HID),
    }


def kernel(x, adj, L0_gnn_Wq, L0_gnn_Wk, L0_gnn_Wv, L0_gnn_Wo, L0_gnn_bo, L0_ffn_router_w,
           L0_ffn_w1, L0_ffn_w2, L0_ffn_w3):
    import numpy as np
    import concourse.bacc as bacc
    from concourse.bass_utils import run_bass_kernel_spmd

    given = (x, adj, L0_gnn_Wq, L0_gnn_Wk, L0_gnn_Wv, L0_gnn_Wo, L0_gnn_bo, L0_ffn_router_w,
             L0_ffn_w1, L0_ffn_w2, L0_ffn_w3)
    arrays = layout(*(np.asarray(a) for a in given))
    nc = bacc.Bacc("TRN2", target_bir_lowering=False, num_devices=1)
    args = {k: nc.dram_tensor(k, a.shape, mybir.dt.from_np(a.dtype), kind="ExternalInput").ap()
            for k, a in arrays.items()}
    out = nc.dram_tensor("out", (GRAPHS, NODES, HID), F32, kind="ExternalOutput").ap()
    build(nc, **args, out=out)
    r = run_bass_kernel_spmd(nc, [arrays], core_ids=[0])
    return r.results[0]["out"]
```

```python
import concourse.bass as bass
from concourse import mybir
from contextlib import ExitStack

F32 = mybir.dt.float32
BF16 = mybir.dt.bfloat16
F32R = mybir.dt.float32r
ALU = mybir.AluOpType
ACT = mybir.ActivationFunctionType
AX = mybir.AxisListType

P = 128
GRAPHS, NODES, HID = 16, 512, 128
HEADS = 8
DH = HID // HEADS
TILES = NODES // P
SLOTS = 16
HALF = SLOTS // 2
GROUP = HEADS // 2
Q_PARTS = (0, 0, 0, 1, 1, 2)
K_PARTS = (0, 1, 2, 0, 1, 0)
ROWS = len(Q_PARTS) * DH
QK_DMAS = 16 * 2 * len(Q_PARTS)
ADJ_EPS = 1e-6
LN_EPS = 1e-5
EXPERTS, TOP = 8, 2
FFN = 341
FT = -(-FFN // P)
TOKENS = GRAPHS * NODES
BLOCK = 256
SUB = BLOCK // P
REGION = TOKENS + BLOCK
N_BLOCKS = TOP * TOKENS // BLOCK + EXPERTS
TRASH = EXPERTS * REGION
DEEP = 4
EARLY = 2
FIRST, TOKEN = HID, HID + 1
WIDE = HID + 2
CONSTANTS = 9
POOL_SLOTS = (1, 3, 5, 7, 9, 11, 13, 15)
RING = 8
LAG = 4
EXPS = 2 * SLOTS
N_POOL = len(POOL_SLOTS)
N_DVE = SLOTS - N_POOL


def pool_made(s):
    return sum(1 for x in POOL_SLOTS if x <= s)


def dve_made(s):
    return s + 1 - pool_made(s)


def wait_alone(eng, m, sem, value):
    if not isinstance(value, int):
        value = eng.to_reg(value)
    if not isinstance(value, int) or value > 0:
        eng.wait_ge(m.ident_ready, 1)
        eng.wait_ge(sem, value)


def wait_pos(eng, s, value):
    if not isinstance(value, int) or value > 0:
        eng.wait_ge(s, value)


class Chain:

    def __init__(self, eng, sem, base):
        self.eng, self.sem, self.base, self.n = eng, sem, base, 0

    def link(self, ins, m=None):
        self.n += 1
        ins.then_inc(self.sem, 1)
        if m is None:
            self.eng.wait_ge(self.sem, self.base + self.n)
        else:
            wait_alone(self.eng, m, self.sem, self.base + self.n)


class Memory:
    pass


def place(nc, ctx):
    m = Memory()

    def sb(name, shape, dt=F32):
        return ctx.enter_context(nc.sbuf_tensor(name, shape, dt))

    def sem(name):
        return ctx.enter_context(nc.semaphore(name))

    m.x = sb("x_all", [P, GRAPHS * TILES, HID])
    m.v = sb("v_all", [P, GRAPHS, TILES * HID])
    m.qs = sb("q_stack", [P, 4, GROUP, NODES], BF16)
    m.ks = sb("k_stack", [P, 4, GROUP, NODES], BF16)
    m.adj = sb("adj_T", [P, 2, TILES, NODES])
    m.qk_loaded = [sem(f"qk_loaded{g}") for g in range(4)]
    m.adj_loaded = [sem(f"adj_loaded{u}") for u in (0, 1)]
    m.vp = sb("v_pad", [P, 2, TILES, HEADS, 32])
    m.ones_ready, m.vp_ready = sem("ones_ready"), sem("v_pad_ready")
    m.ident = sb("ident", [P, P])
    m.wq, m.wk, m.wv, m.wo = (sb(n, [P, HID]) for n in ("wqT", "wkT", "wvT", "woT"))
    m.bo = sb("bo_rows", [P, HID])
    m.router = sb("routerT", [P, EXPERTS])
    m.before = sb("before_me", [P, P])
    m.ones = sb("all_ones", [P, P])
    m.small = sb("small_constants", [P, 2 * EXPERTS + TILES])
    m.blocks = sb("block_numbers", [P, N_BLOCKS])
    m.gates = sb("gates", [P, GRAPHS * TILES, TOP])
    m.counts = sb("seen_before", [P, TILES + 1, EXPERTS])
    m.psum = ctx.enter_context(nc.psum_tensor("psum", [P, 8, 512], F32))
    m.xr = sb("block_rows", [P, DEEP, SUB, WIDE])
    m.w13 = sb("w13_block", [P, DEEP, 2, FT, P])
    m.w2 = sb("w2_block", [P, DEEP, FT, HID])
    m.number = sb("expert_of_block_f", [P, N_BLOCKS])
    m.exp_i = sb("expert_of_block", [1, N_BLOCKS], mybir.dt.uint32)
    m.src_i = sb("read_row", [1, N_BLOCKS], mybir.dt.uint32)
    m.w13_loaded = [sem(f"w13_loaded{q}") for q in range(DEEP)]
    m.w2_loaded = [sem(f"w2_loaded{q}") for q in range(DEEP)]
    m.const_in = sem("const_in")
    m.ident_ready = sem("ident_ready")
    return m


def load_stacks(sp, m, qk_d, b, u, g):
    buf = 2 * u + g
    cols = slice(g * GROUP * NODES, (g + 1) * GROUP * NODES)
    for stack, first, order in ((m.qs, 0, Q_PARTS), (m.ks, 3, K_PARTS)):
        for j, part in enumerate(order):
            src = qk_d[b, first + part, :, :].rearrange("(d h) c -> d (h c)", d=DH)
            sp.dma_start(stack[DH * j:DH * (j + 1), buf, :, :].rearrange("d h c -> d (h c)"),
                         src[:, cols]).then_inc(m.qk_loaded[buf], 16)


def stage_projections(nc, m, x_d, w_d, qk_d, adj_d):
    with ExitStack() as ctx:
        def sb(name, shape, dt=F32):
            return ctx.enter_context(nc.sbuf_tensor(name, shape, dt))

        def sem(name):
            return ctx.enter_context(nc.semaphore(name))

        stats = sb("ln_stats", [P, 2, TILES, 6])
        mv = sb("ln_mean_var", [P, 2, TILES, 2])
        var_eps = sb("ln_var_eps", [P, 2, TILES])
        minus_half = sb("minus_half", [P, TILES])
        rstd = sb("ln_rstd", [P, 2, TILES])
        xn = sb("xn", [P, 2, TILES, HID])
        xnT = sb("xnT", [P, 2, NODES])
        parts = sb("qk_parts", [P, 2, 6, NODES], BF16)
        rest = sb("qk_rest", [P, 2, 2, NODES])

        x_in, x_landed = [sem("x_in0"), sem("x_in1")], sem("x_landed")
        half_ready, stats_ready, mv_ready = sem("half_ready"), sem("stats_ready"), sem("mv_ready")
        var_ready, rstd_ready = sem("var_ready"), sem("rstd_ready")
        xn_ready, xnT_psum, xnT_ready = sem("xn_ready"), sem("xnT_psum"), sem("xnT_ready")
        q_psum, k_psum, v_psum = sem("q_psum"), sem("k_psum"), sem("v_psum")
        high_ready, rest_ready, mid_ready = sem("high_ready"), sem("rest_ready"), sem("mid_ready")
        low_ready, v_ready, biased = sem("low_ready"), sem("v_ready"), sem("residual_biased")
        stored = [sem("stacks_stored0"), sem("stacks_stored1")]
        AHEAD = 3

        def every_graph(body):
            def walk(eng):
                with eng.Fori(0, GRAPHS // 2 - 3) as n:
                    for u in (0, 1):
                        body(2 * n + u, n, u)
                for b in range(GRAPHS - 6, GRAPHS):
                    body(b, b // 2, b % 2)
            return walk

        def exists(b):
            return not isinstance(b, int) or b < GRAPHS

        with nc.Block() as block:
            @block.sync
            def _(sp):
                def load(b, u):
                    sp.dma_start(m.x[:, bass.ds(b * TILES, TILES), :],
                                 x_d[b, :, :].rearrange("(t p) c -> p t c", p=P)).then_inc(x_in[u], 16)

                def landed(n, u):
                    sp.wait_ge(x_in[u], 16 * n + 16)
                    sp.sem_inc(x_landed, 1)

                load(0, 0)
                load(1, 1)
                for t, d in ((m.wq, w_d[0]), (m.wk, w_d[1]), (m.wv, w_d[2]), (m.wo, w_d[3]),
                             (m.bo, w_d[4]), (m.router, w_d[5]), (m.before, w_d[6]),
                             (m.small, w_d[7]), (m.blocks, w_d[8])):
                    sp.dma_start(t[:, :], d).then_inc(m.const_in, 16)
                for b in range(AHEAD):
                    landed(b // 2, b % 2)
                    load(b + 2, b % 2)

                def body(b, n, u):
                    if exists(b + AHEAD):
                        landed(n + (u + AHEAD) // 2, (u + AHEAD) % 2)
                    if exists(b + AHEAD + 2):
                        load(b + AHEAD + 2, (u + AHEAD) % 2)
                    sp.wait_ge(low_ready, 2 * b + 2 + 4)
                    sp.dma_start(qk_d[b, :, :, :].rearrange("s p c -> p s c"),
                                 parts[:, u, :, :]).then_inc(stored[u], 16)
                    if isinstance(b, int) and b in (GRAPHS - 4, GRAPHS - 2):
                        sp.wait_ge(stored[0], 16 * n + 16)
                        load_stacks(sp, m, qk_d, 0, 0, (b - GRAPHS + 4) // 2)
                every_graph(body)(sp)
                sp.dma_start(m.adj[:, 0, :, :], adj_d[0, :, :].rearrange("(t p) q -> p t q", p=P)
                             ).then_inc(m.adj_loaded[0], 16)
                for u in (0, 1):
                    sp.wait_ge(stored[u], 16 * (GRAPHS // 2) + 16)

            @block.gpsimd
            def _(pool):
                pool.memset(m.ident[:, :], 0.0).then_inc(m.ident_ready, 1)
                pool.wait_ge(m.ident_ready, 1)
                pool.affine_select(out=m.ident[:, :], in_=m.ident[:, :], compare_op=ALU.not_equal,
                                   fill=1.0, base=0, pattern=[[-1, P]], channel_multiplier=1
                                   ).then_inc(m.ident_ready, 1)
                pool.memset(m.ones[:, :], 1.0).then_inc(half_ready, 1)
                pool.memset(m.counts[:, :, :], 0.0).then_inc(half_ready, 1)
                pool.memset(minus_half[:, :], -0.5).then_inc(half_ready, 1)
                pool.wait_ge(half_ready, 3)
                pool.sem_inc(m.ones_ready, 1)

                def invert(b, u):
                    pool.wait_ge(var_ready, b + 1)
                    pool.tensor_tensor(rstd[:, u, :], var_eps[:, u, :], minus_half[:, :],
                                       ALU.pow).then_inc(rstd_ready, 1)

                def body(b, n, u):
                    for j in range(2):
                        pool.wait_ge(mid_ready, 2 * b + j + 1)
                        pool.tensor_tensor(parts[:, u, 3 * j + 2, :], rest[:, u, j, :],
                                           parts[:, u, 3 * j + 1, :], ALU.subtract).then_inc(low_ready, 1)
                    xb = m.x[:, bass.ds(b * TILES, TILES), :]
                    pool.tensor_tensor(xb, xb, m.bo[:, :].unsqueeze(1).to_broadcast([P, TILES, HID]),
                                       ALU.add).then_inc(biased, 1)
                    if exists(b + AHEAD):
                        invert(b + AHEAD, (u + AHEAD) % 2)

                for b in range(AHEAD):
                    invert(b, b % 2)
                pool.wait_ge(m.const_in, CONSTANTS * 16)
                every_graph(body)(pool)
                pool.wait_ge(biased, GRAPHS)

            @block.vector
            def _(dve):
                def statistics(b, u, k):
                    if k == 0:
                        wait_alone(dve, m, x_landed, b + 1)
                        for t in range(TILES):
                            last = dve.bn_stats(stats[:, u, t, :], m.x[:, b * TILES + t, :])
                        last.then_inc(stats_ready, 1)
                    if k == 1:
                        wait_alone(dve, m, stats_ready, b + 1)
                        for t in range(TILES):
                            last = dve.bn_aggr(mv[:, u, t, :], stats[:, u, t, :])
                        last.then_inc(mv_ready, 1)
                    if k == 2:
                        dve.wait_ge(mv_ready, b + 1)
                        dve.tensor_scalar_add(var_eps[:, u, :], mv[:, u, :, 1], LN_EPS
                                              ).then_inc(var_ready, 1)

                def norm(b, u):
                    dve.wait_ge(rstd_ready, b + 1)
                    wait_pos(dve, xnT_psum, b - 1)
                    for t in range(TILES):
                        last = dve.tensor_scalar(xn[:, u, t, :], m.x[:, b * TILES + t, :],
                                                 mv[:, u, t, 0:1], rstd[:, u, t:t + 1],
                                                 ALU.subtract, ALU.mult)
                    last.then_inc(xn_ready, 1)

                def split_rest(b, u, j):
                    dve.wait_ge(high_ready, 2 * b + j + 1)
                    dve.wait_ge(low_ready, 2 * b + j + 1)
                    dve.tensor_tensor(rest[:, u, j, :], m.psum[:, 2 + 2 * j + u, :],
                                      parts[:, u, 3 * j, :], ALU.subtract).then_inc(rest_ready, 1)

                def split_mid(b, u, j):
                    dve.wait_ge(rest_ready, 2 * b + j + 1 + 4)
                    dve.tensor_copy(parts[:, u, 3 * j + 1, :], rest[:, u, j, :]).then_inc(mid_ready, 1)

                dve.memset(m.vp[:, :, :, :, :], 0.0).then_inc(m.vp_ready, 1)
                dve.wait_ge(m.vp_ready, 1)
                dve.memset(m.vp[:, :, :, :, DH:DH + 1], 1.0).then_inc(m.vp_ready, 1)
                dve.sem_inc(low_ready, 4)
                dve.sem_inc(rest_ready, 4)
                for b in range(AHEAD):
                    for k in range(3):
                        statistics(b, b % 2, k)
                    if b < AHEAD - 1:
                        norm(b, b % 2)

                def body(b, n, u):
                    far, v = exists(b + AHEAD), (u + AHEAD) % 2
                    split_rest(b, u, 0)
                    if far:
                        statistics(b + AHEAD, v, 0)
                    split_mid(b, u, 0)
                    split_rest(b, u, 1)
                    if far:
                        statistics(b + AHEAD, v, 1)
                    split_mid(b, u, 1)
                    if far:
                        statistics(b + AHEAD, v, 2)
                    if exists(b + AHEAD - 1):
                        norm(b + AHEAD - 1, u)
                every_graph(body)(dve)

            @block.tensor
            def _(pe):
                pe.wait_ge(m.ident_ready, 2)
                pe.wait_ge(m.const_in, CONSTANTS * 16)

                def turn(b, u):
                    pe.wait_ge(xn_ready, b + 1)
                    for t in range(TILES):
                        last = pe.transpose(m.psum[:, u, t * P:(t + 1) * P], xn[:, u, t, :], m.ident[:, :])
                    last.then_inc(xnT_psum, 1)

                def body(b, n, u):
                    pe.wait_ge(xnT_ready, b + 1)
                    pe.wait_ge(rest_ready, 2 * b + 1)
                    pe.matmul(m.psum[:, 2 + u, :], m.wq[:, :], xnT[:, u, :],
                              start=True, stop=True).then_inc(q_psum, 1)
                    pe.wait_ge(rest_ready, 2 * b + 2)
                    pe.matmul(m.psum[:, 4 + u, :], m.wk[:, :], xnT[:, u, :],
                              start=True, stop=True).then_inc(k_psum, 1)
                    if exists(b + 1):
                        turn(b + 1, 1 - u)
                    pe.wait_ge(v_ready, b + 1)
                    for t in range(TILES):
                        last = pe.matmul(m.psum[:, 6 + u, t * P:(t + 1) * P],
                                         xnT[:, u, t * P:(t + 1) * P], m.wv[:, :], start=True, stop=True)
                    last.then_inc(v_psum, 1)
                turn(0, 0)
                every_graph(body)(pe)

            @block.scalar
            def _(act):
                act.sem_inc(v_ready, 2)
                act.sem_inc(stored[0], 16)
                act.sem_inc(stored[1], 16)

                def turned(b, u):
                    act.wait_ge(xnT_psum, b + 1)
                    wait_pos(act, v_psum, b - 1)
                    act.copy(xnT[:, u, :], m.psum[:, u, :]).then_inc(xnT_ready, 1)

                def body(b, n, u):
                    act.wait_ge(stored[u], 16 * n + 16)
                    act.wait_ge(q_psum, b + 1)
                    act.copy(parts[:, u, 0, :], m.psum[:, 2 + u, :]).then_inc(high_ready, 1)
                    act.wait_ge(k_psum, b + 1)
                    act.copy(parts[:, u, 3, :], m.psum[:, 4 + u, :]).then_inc(high_ready, 1)
                    if exists(b + 1):
                        turned(b + 1, 1 - u)
                    act.wait_ge(v_psum, b + 1)
                    act.copy(m.v[:, b, :], m.psum[:, 6 + u, :]).then_inc(v_ready, 1)
                act.wait_ge(m.ones_ready, 1)
                act.copy(m.ks[ROWS:ROWS + 3, :, :, :].rearrange("p g h c -> p (g h c)"),
                         m.ones[ROWS:ROWS + 3, 0:1].to_broadcast([3, 4 * GROUP * NODES])
                         ).then_inc(m.ones_ready, 1)
                turned(0, 0)
                every_graph(body)(act)


def expert(sp, m, j):
    return sp.value_load(m.exp_i[0:1, bass.ds(j, 1)], min_val=0, max_val=EXPERTS - 1)


def w13_in(sp, m, w13_d, e, q):
    sp.dma_start(m.w13[:, q, :, :, :].rearrange("p a t h -> p (a t h)"),
                 w13_d[bass.ds(e, 1), :, :].squeeze(0)).then_inc(m.w13_loaded[q], 16)


def w2_in(sp, m, w2_d, e, q):
    sp.dma_start(m.w2[:, q, :, :].rearrange("p t c -> p (t c)"),
                 w2_d[bass.ds(e, 1), :, :].squeeze(0)).then_inc(m.w2_loaded[q], 16)


class Tables:

    def __init__(self, nc, ctx, m, rows_d, w13_d, w2_d):
        def sb(name, shape, dt=F32):
            return ctx.enter_context(nc.sbuf_tensor(name, shape, dt))

        E, NB, I32 = EXPERTS, N_BLOCKS, mybir.dt.int32
        self.m, self.rows_d, self.w13_d, self.w2_d = m, rows_d, w13_d, w2_d
        self.empty = sb("empty_rows", [P, SUB, WIDE])
        self.count = sb("expert_count", [P, E])
        self.full = sb("expert_blocks_int", [P, 2, E], I32)
        self.many = sb("expert_blocks", [P, E])
        self.none = sb("no_blocks", [P, E])
        self.last_b = sb("blocks_up_to", [P, E])
        self.first_b = sb("first_block", [P, E])
        self.past = sb("past_expert", [P, NB, E])
        self.begun = sb("begun_expert", [1, NB, E])
        self.where = sb("row_if_expert", [1, NB, E])
        self.spill = sb("is_trash", [1, NB])
        self.src_f, self.end_f = sb("read_row_f", [1, NB]), sb("end_row_f", [1, E])
        self.end_i = sb("end_row", [1, E], mybir.dt.uint32)
        self.e_ready, self.cnt_psum, self.chain, self.ends_ready, self.tab_ready, self.ends = (
            ctx.enter_context(nc.semaphore(n)) for n in (
                "empty_rows_ready", "counts_summed", "table_chain", "ends_ready", "table_ready",
                "region_ends_emptied"))

    def empty_rows(self, pool):
        m, empty = self.m, self.empty
        pool.memset(empty[:, :, 0:FIRST], 0.0)
        pool.memset(empty[:, :, FIRST:TOKEN], -1.0)
        pool.tensor_scalar(empty[:, :, TOKEN], m.small[:, 2 * EXPERTS:2 * EXPERTS + SUB],
                           float(TOKENS), 1.0, ALU.add, ALU.mult).then_inc(self.e_ready, 1)

    def tensor(self, pe):
        pe.matmul(self.m.psum[:, 2, 0:EXPERTS], self.m.ones[:, :], self.m.counts[:, TILES, :],
                  start=True, stop=True).then_inc(self.cnt_psum, 1)

    def vector(self, dve):
        m, E, NB = self.m, EXPERTS, N_BLOCKS
        count, full, many, none, last_b, first_b = (
            self.count, self.full, self.many, self.none, self.last_b, self.first_b)
        past, begun, where, spill, src_f, end_f = (
            self.past, self.begun, self.where, self.spill, self.src_f, self.end_f)
        L = Chain(dve, self.chain, 0).link
        dve.wait_ge(self.cnt_psum, 1)
        L(dve.tensor_copy(count[:, :], m.psum[:, 2, 0:E]))
        L(dve.tensor_tensor(end_f[:, :], m.small[0:1, E:2 * E], count[0:1, :], ALU.add))
        dve.tensor_copy(self.end_i[:, :], end_f[:, :]).then_inc(self.ends_ready, 1)
        L(dve.tensor_scalar_add(full[:, 0, :], count[:, :], float(BLOCK - 1)))
        L(dve.tensor_single_scalar(full[:, 1, :], full[:, 0, :], BLOCK.bit_length() - 1,
                                   ALU.arith_shift_right))
        L(dve.tensor_copy(many[:, :], full[:, 1, :]))
        L(dve.memset(none[:, :], 0.0))
        L(dve.tensor_tensor_scan(last_b[:, :], many[:, :], none[:, :], 0.0, ALU.add, ALU.add))
        L(dve.tensor_tensor(first_b[:, :], last_b[:, :], many[:, :], ALU.subtract))
        nb = m.blocks[0:1, :].unsqueeze(2).to_broadcast([1, NB, E])

        def per_expert(a):
            return a.unsqueeze(1).to_broadcast([1, NB, E])
        L(dve.tensor_tensor(past[:, :, :], m.blocks[:, :].unsqueeze(2).to_broadcast([P, NB, E]),
                            last_b[:, :].unsqueeze(1).to_broadcast([P, NB, E]), ALU.is_ge))
        L(dve.tensor_reduce(m.number[:, :], past[:, :, :], AX.X, ALU.add))
        L(dve.tensor_scalar(spill[:, :], m.number[0:1, :], float(E), float(TRASH), ALU.is_ge, ALU.mult))
        L(dve.tensor_scalar(m.number[:, :], m.number[:, :], float(E - 1), None, ALU.min))
        dve.tensor_copy(m.exp_i[:, :], m.number[0:1, :]).then_inc(self.tab_ready, 1)
        L(dve.tensor_tensor(begun[:, :, :], nb, per_expert(first_b[0:1, :]), ALU.is_ge))
        L(dve.tensor_tensor(begun[:, :, :], begun[:, :, :], past[0:1, :, :], ALU.subtract))
        L(dve.tensor_tensor(where[:, :, :], nb, per_expert(first_b[0:1, :]), ALU.subtract))
        L(dve.tensor_scalar(where[:, :, :], where[:, :, :], float(BLOCK), None, ALU.mult))
        L(dve.tensor_tensor(where[:, :, :], where[:, :, :], per_expert(m.small[0:1, E:2 * E]), ALU.add))
        L(dve.tensor_tensor(where[:, :, :], where[:, :, :], begun[:, :, :], ALU.mult))
        L(dve.tensor_reduce(src_f[:, :], where[:, :, :], AX.X, ALU.add))
        L(dve.tensor_tensor(src_f[:, :], src_f[:, :], spill[:, :], ALU.add))
        dve.tensor_copy(m.src_i[:, :], src_f[:, :]).then_inc(self.tab_ready, 1)

    def sync(self, sp):
        sp.wait_ge(self.e_ready, 1)
        sp.wait_ge(self.ends_ready, 1)

        def to_empty(row):
            sp.dma_start(self.rows_d[bass.ds(row, BLOCK), :].rearrange("(p s) c -> p s c", s=SUB),
                         self.empty[:, :, :]).then_inc(self.ends, 16)
        for e in range(EXPERTS):
            to_empty(sp.value_load(self.end_i[0:1, e:e + 1], min_val=0, max_val=TRASH - BLOCK))
        to_empty(TRASH)
        sp.wait_ge(self.tab_ready, 1)
        for q in range(EARLY):
            w13_in(sp, self.m, self.w13_d, expert(sp, self.m, q), q)
        sp.wait_ge(self.ends, 16 * (EXPERTS + 1))
        sp.wait_ge(self.tab_ready, 2)


def stage_attention(nc, m, adj_d, qk_d, rows_d, w13_d, w2_d):
    with ExitStack() as ctx:
        def sb(name, shape, dt=F32):
            return ctx.enter_context(nc.sbuf_tensor(name, shape, dt))

        def sem(name):
            return ctx.enter_context(nc.semaphore(name))

        qs, ks, vp, adj = m.qs, m.ks, m.vp, m.adj
        ex = sb("weights", [P, RING, 2, NODES])
        mx = sb("minus_max", [P, 4, 16])
        mx_parts = sb("minus_max_parts", [16, 2, 3, P], BF16)
        mx_rest = sb("minus_max_rest", [16, 2, P])
        osb = sb("values_T", [P, NODES])
        rec = sb("row_sum_inverse", [P, TILES, GROUP])
        an = sb("attended", [P, TILES, HID])
        anT = sb("attended_T", [P, NODES])

        stats = sb("ln2_stats", [P, TILES, 6])
        mv = sb("ln2_mean_var", [P, TILES, 2])
        var_eps = sb("ln2_var_eps", [P, TILES])
        minus_half = sb("ln2_minus_half", [P, TILES])
        rstd = sb("ln2_rstd", [P, TILES])
        minus_mean = sb("ln2_minus_mean_rstd", [P, TILES])
        xn = sb("xn2", [P, 2, TILES, WIDE])
        xnT = sb("xn2_T", [P, NODES])
        lmax = sb("minus_max_logit", [P, TILES])
        prob = sb("router_probs", [P, TILES, EXPERTS])
        psum_inv = sb("prob_sum", [P, 2, TILES])
        top = sb("top_probs", [P, TILES, 8])
        topi = sb("top_experts", [P, TILES, 8], mybir.dt.uint32)
        topf = sb("chosen_experts", [P, TILES, TOP])
        tsum = sb("top_sum", [P, 2, TILES])
        hot = sb("choice_one_hot", [P, TILES, TOP, EXPERTS])
        given = sb("given_to", [P, TILES, EXPERTS])
        rank = sb("rank_rows", [P, TILES, EXPERTS])
        picked = sb("rank_picked", [P, TILES, TOP, EXPERTS])
        posf = sb("row_float", [P, TILES, TOP])
        pos2 = sb("row_index", [P, 2, TILES, TOP], mybir.dt.uint32)

        stats_ready, mv_ready = sem("ln2_stats_ready"), sem("ln2_mv_ready")
        var_ready, rstd_ready, xn_ready = sem("ln2_var_ready"), sem("ln2_rstd_ready"), sem("xn2_ready")
        shift_ready = sem("ln2_shift_ready")
        xnT_psum, xnT_ready = sem("xn2_turned"), sem("xn2_T_ready")
        lmax_ready, lg_psum, lg_read = sem("max_logit_ready"), sem("logits_ready"), sem("logits_read")
        prob_exp, chosen = sem("probs_exp"), sem("choice_steps")
        rank_psum, rank_read = sem("ranks_ready"), sem("ranks_read")
        picked_ready, posf_ready = sem("picked_ready"), sem("row_float_ready")
        pos_ready, scattered = sem("rows_ready"), [sem("scattered0"), sem("scattered1")]
        half_ready = sem("ln2_half_ready")
        qk_loaded, adj_loaded = m.qk_loaded, m.adj_loaded
        shift_loaded = [sem(f"shift_loaded{g}") for g in range(4)]
        v_placed = sem("v_placed")
        adj_ready = sem("adj_eps_added")
        st_ready, exp_ready = sem("scores_ready"), sem("exp_ready")
        sm_ready, max_done = sem("scores_for_max"), sem("max_done")
        made_dve, made_pool = sem("products_of_dve"), sem("products_of_pool")
        pv_done, osb_ready = sem("values_summed"), sem("values_copied")
        mt_psum, mt_high, mt_rest, mt_mid, mt_low = (sem(n) for n in (
            "max_turned", "max_high", "max_rest", "max_mid", "max_low"))
        ot_psum, rec_ready, an_ready = sem("values_turned"), sem("sums_inverted"), sem("attended_ready")
        at_psum, at_ready = sem("attended_turned"), sem("attended_T_ready")
        wo_psum, x1_ready = sem("output_ready"), sem("x1_ready")

        ST = [m.psum[:, 0, :], m.psum[:, 1, :]]
        SM = [m.psum[:, 2:4, :], m.psum[:, 4:6, :]]
        OT = m.psum[:, 6, :]
        MISC = m.psum[:, 7, :]
        CHOICE_AT = ((2, 0), (2, 1), (3, 0), (4, 0), (4, 1), (5, 0),
                     (6, 0), (6, 1), (7, 0), (8, 0), (8, 1), (9, 0))
        CHOICE = len(CHOICE_AT)
        STATS_AT = ((9, 0), (10, 0), (10, 1))
        PICK_AT = ((10, 0), (10, 1), (11, 0), (12, 0))
        RANKS = MISC[:, P:P + TILES * EXPERTS]

        def every_window(body):
            def walk(eng):
                body(-1, -1, 1, False, True, False, False, False)
                body(0, 0, 0, True, True, False, False, False)
                body(1, 0, 1, True, True, True, False, False)
                body(2, 1, 0, True, True, True, True, False)
                body(3, 1, 1, True, True, True, True, True)
                with eng.Fori(0, GRAPHS // 2 - 3) as i:
                    body(2 * i + 4, i + 2, 0, True, True, True, True, True)
                    body(2 * i + 5, i + 2, 1, True, True, True, True, True)
                body(GRAPHS - 2, GRAPHS // 2 - 1, 0, True, True, True, True, True)
                body(GRAPHS - 1, GRAPHS // 2 - 1, 1, True, False, True, True, True)
                body(GRAPHS, GRAPHS // 2, 0, False, False, True, True, True)
                body(GRAPHS + 1, GRAPHS // 2, 1, False, False, False, True, True)
                body(GRAPHS + 2, GRAPHS // 2 + 1, 0, False, False, False, False, True)
            return walk

        tables = Tables(nc, ctx, m, rows_d, w13_d, w2_d)

        with nc.Block() as block:
            @block.sync
            def _(sp):
                def load_group(b, n, u, g):
                    wait_pos(sp, qk_loaded[2 * u + g], QK_DMAS * n)
                    load_stacks(sp, m, qk_d, b, u, g)

                def load_adj(b, u):
                    sp.dma_start(adj[:, u, :, :], adj_d[b, :, :].rearrange("(t p) q -> p t q", p=P)
                                 ).then_inc(adj_loaded[u], 16)

                def load_shift(b, u, g):
                    sp.wait_ge(mt_low, 2 * b + g + 1)
                    for part in range(3):
                        sp.dma_start(qs[ROWS + part:ROWS + part + 1, 2 * u + g, :, :].rearrange(
                                         "o h (t p) -> o (h t) p", p=P),
                                     mx_parts[:, g, part, :]
                                     ).then_inc(shift_loaded[2 * u + g], 16)

                def body(b, n, u, scores, maxima, tail, route, rows):
                    v, nv = 1 - u, n + u
                    if maxima:
                        wait_pos(sp, st_ready, EXPS * b)
                        if scores:
                            load_group(b + 1, nv, v, 1)
                        if scores:
                            wait_alone(sp, m, made_dve, N_DVE * b)
                            wait_pos(sp, made_pool, N_POOL * b)
                            load_adj(b + 1, v)
                    if scores:
                        load_shift(b, u, 1)
                    if maxima:
                        if not isinstance(b, int) or b < GRAPHS - 2:
                            if scores:
                                sp.wait_ge(st_ready, EXPS * b + EXPS // 2)
                            load_group(b + 2, n + 1, u, 0)
                        load_shift(b + 1, v, 0)

                every_window(body)(sp)
                tables.sync(sp)

            @block.gpsimd
            def _(pool):
                pool.memset(minus_half[:, :], -0.5).then_inc(half_ready, 1)
                pool.wait_ge(half_ready, 1)
                tables.empty_rows(pool)

                def product(b, u, s):
                    if s == POOL_SLOTS[0]:
                        pool.wait_ge(adj_ready, b + 1)
                    pool.wait_ge(exp_ready, EXPS * b + 2 * s + 2)
                    pool.tensor_tensor(ex[:, s % RING, :, :], ex[:, s % RING, :, :],
                                       adj[:, u, s % HALF // 2, :].unsqueeze(1).to_broadcast([P, 2, NODES]),
                                       ALU.mult).then_inc(made_pool, 1)

                def scatter(c, cu, i):
                    if i == 0:
                        wait_alone(pool, m, pos_ready, c + 1)
                    t, k = i // TOP, i % TOP
                    pool.indirect_dma_start(
                        rows_d[:, :], bass.IndirectOffsetOnAxis(ap=pos2[:, cu, t, k:k + 1], axis=0),
                        xn[:, cu, t, :], None).then_inc(scattered[cu], 16)

                def body(b, n, u, scores, maxima, tail, route, rows):
                    v, nv = 1 - u, n + u
                    for s in range(SLOTS):
                        if scores and s in POOL_SLOTS:
                            product(b, u, s)
                        if rows and s < TILES * TOP:
                            scatter(b - 3, 1 - u, s)
                        if maxima and s == 8:
                            wait_alone(pool, m, adj_loaded[v], 16 * nv + 16)
                            pool.tensor_scalar(adj[:, v, :, :], adj[:, v, :, :], ADJ_EPS, 1.0,
                                               ALU.add, ALU.mult).then_inc(adj_ready, 1)
                        if tail and s == 11:
                            pool.wait_ge(var_ready, b)
                            pool.tensor_tensor(rstd[:, :], var_eps[:, :], minus_half[:, :],
                                               ALU.pow).then_inc(rstd_ready, 1)
                every_window(body)(pool)
                for u in (0, 1):
                    pool.wait_ge(scattered[u], 16 * TILES * TOP * GRAPHS // 2)

            @block.scalar
            def _(act):
                def values_copy(b, g):
                    act.wait_ge(pv_done, HALF * b + 4 * g + 4)
                    wait_pos(act, ot_psum, 2 * b + g)
                    act.copy(osb[:, :], OT).then_inc(osb_ready, 1)

                def max_high(b, g):
                    act.wait_ge(mt_psum, 2 * b + g + 1)
                    act.copy(mx_parts[:, g, 0, :], MISC[0:16, 0:P]).then_inc(mt_high, 1)

                def norm(c, cn, cu):
                    wait_alone(act, m, scattered[cu], 16 * TILES * TOP * cn)
                    wait_alone(act, m, shift_ready, c + 1)
                    for t in range(TILES):
                        last = act.activation(xn[:, cu, t, 0:HID], m.x[:, c * TILES + t, :], ACT.Identity,
                                              bias=minus_mean[:, t:t + 1], scale=rstd[:, t:t + 1])
                    last.then_inc(xn_ready, 1)

                def place_v(b, u):
                    wait_pos(act, pv_done, HALF * (b - 1))
                    act.copy(vp[:, u, :, :, 0:DH],
                             m.v[:, b, :].rearrange("p (t h d) -> p t h d", t=TILES, h=HEADS)
                             ).then_inc(v_placed, 1)

                def body(b, n, u, scores, maxima, tail, route, rows):
                    for s in range(SLOTS):
                        if scores:
                            if s % 2 == 0:
                                wait_pos(act, pv_done, HALF * b + (s - RING) // 2 + 1)
                            for h in (0, 1):
                                act.wait_ge(st_ready, EXPS * b + 2 * s + h + 1)
                                act.activation(ex[:, s % RING, h, :], ST[h], ACT.Exp, scale=DH ** -0.5
                                               ).then_inc(exp_ready, 1)
                        if s == 0 and route:
                            act.wait_ge(xnT_psum, b - 1)
                            wait_pos(act, lg_psum, b - 2)
                            act.copy(xnT[:, :], MISC).then_inc(xnT_ready, 1)
                        if s == 3 and tail:
                            values_copy(b - 1, 1)
                        if s == 3 and scores:
                            max_high(b, 1)
                        if s == 3 and route:
                            act.wait_ge(lg_read, b - 1)
                            act.activation(prob[:, :, :], prob[:, :, :], ACT.Exp).then_inc(prob_exp, 1)
                        if s == 5 and maxima:
                            place_v(b + 1, 1 - u)
                        if s == 7 and tail:
                            act.wait_ge(at_psum, b)
                            wait_pos(act, wo_psum, b - 1)
                            act.copy(anT[:, :], MISC).then_inc(at_ready, 1)
                        if s == 9 and tail:
                            act.wait_ge(wo_psum, b)
                            act.copy(m.x[:, bass.ds((b - 1) * TILES, TILES), :],
                                     MISC.rearrange("p (t c) -> p t c", t=TILES)).then_inc(x1_ready, 1)
                        if s == 13 and tail:
                            norm(b - 1, n - (1 - u), 1 - u)
                        if s == 11 and maxima:
                            max_high(b + 1, 0)
                        if s == 11 and scores:
                            values_copy(b, 0)
                every_window(body)(act)

            @block.vector
            def _(dve):
                for u in (0, 1):
                    dve.tensor_scalar_add(xn[:, u, :, TOKEN], m.small[:, 2 * EXPERTS:],
                                          float((u - 2) * NODES))

                def low_parts(b, g, k):
                    i = 2 * b + g
                    if k == 0:
                        dve.wait_ge(mt_high, i + 1)
                        dve.tensor_tensor(mx_rest[:, g, :], MISC[0:16, 0:P], mx_parts[:, g, 0, :],
                                          ALU.subtract).then_inc(mt_rest, 1)
                    if k == 1:
                        dve.wait_ge(mt_rest, i + 1)
                        dve.tensor_copy(mx_parts[:, g, 1, :], mx_rest[:, g, :]).then_inc(mt_mid, 1)
                    if k == 2:
                        dve.wait_ge(mt_mid, i + 1)
                        dve.tensor_tensor(mx_parts[:, g, 2, :], mx_rest[:, g, :], mx_parts[:, g, 1, :],
                                          ALU.subtract).then_inc(mt_low, 1)

                def normalise(b, g, k):
                    i = 2 * b + g
                    t = MISC.rearrange("p (t j c) -> p t j c", t=TILES, c=32)
                    if k == 0:
                        dve.wait_ge(ot_psum, i + 1)
                        dve.reciprocal(rec[:, :, :], t[:, :, :, DH]).then_inc(rec_ready, 1)
                    if k == 1:
                        dve.wait_ge(rec_ready, i + 1)
                        if g == 0:
                            wait_pos(dve, at_psum, b)
                        out = an[:, :, g * 64:g * 64 + 64].rearrange("p t (j d) -> p t j d", d=DH)
                        dve.tensor_tensor(out, t[:, :, :, 0:DH],
                                          rec[:, :, :].unsqueeze(3).to_broadcast([P, TILES, GROUP, DH]),
                                          ALU.mult).then_inc(an_ready, 1)

                def norm_stats(c, k):
                    if k == 0:
                        wait_alone(dve, m, x1_ready, c + 1)
                        for t in range(TILES):
                            last = dve.bn_stats(stats[:, t, :], m.x[:, c * TILES + t, :])
                        last.then_inc(stats_ready, 1)
                    if k == 1:
                        wait_alone(dve, m, stats_ready, c + 1)
                        for t in range(TILES):
                            last = dve.bn_aggr(mv[:, t, :], stats[:, t, :])
                        last.then_inc(mv_ready, 1)
                    if k == 2:
                        dve.wait_ge(mv_ready, c + 1)
                        dve.tensor_scalar_add(var_eps[:, :], mv[:, :, 1], LN_EPS).then_inc(var_ready, 1)

                def norm_shift(c):
                    dve.wait_ge(rstd_ready, c + 1)
                    dve.scalar_tensor_tensor(minus_mean[:, :], mv[:, :, 0], -1.0, rstd[:, :],
                                             ALU.mult, ALU.mult).then_inc(shift_ready, 1)

                lg = MISC[:, 0:TILES * EXPERTS].rearrange("p (t e) -> p t e", e=EXPERTS)

                def shift_logits(c, k):
                    if k == 0:
                        dve.wait_ge(lg_psum, c + 1)
                        dve.tensor_reduce(lmax[:, :], lg, AX.X, ALU.max, negate=True
                                          ).then_inc(lmax_ready, 1)
                    if k == 1:
                        dve.wait_ge(lmax_ready, c + 1)
                        dve.tensor_tensor(prob[:, :, :], lg,
                                          lmax[:, :].unsqueeze(2).to_broadcast([P, TILES, EXPERTS]),
                                          ALU.add).then_inc(lg_read, 1)

                def choose(c, cu, k):
                    if k == 0:
                        dve.wait_ge(prob_exp, c + 1)
                        last = dve.tensor_reduce(psum_inv[:, 0, :], prob[:, :, :], AX.X, ALU.add)
                    elif k in (3, 4):
                        wait_alone(dve, m, chosen, CHOICE * c + k)
                    else:
                        dve.wait_ge(chosen, CHOICE * c + k)
                    if k == 1:
                        last = dve.reciprocal(psum_inv[:, 1, :], psum_inv[:, 0, :])
                    if k == 2:
                        last = dve.tensor_tensor(
                            prob[:, :, :], prob[:, :, :],
                            psum_inv[:, 1, :].unsqueeze(2).to_broadcast([P, TILES, EXPERTS]), ALU.mult)
                    if k == 3:
                        for t in range(TILES):
                            last = dve.max(top[:, t, :], prob[:, t, :])
                    if k == 4:
                        for t in range(TILES):
                            last = dve.max_index(topi[:, t, :], top[:, t, :], prob[:, t, :])
                    if k == 5:
                        dve.tensor_copy(topf[:, :, :], topi[:, :, 0:TOP])
                        dve.tensor_copy(xn[:, cu, :, FIRST], topi[:, :, 0])
                        dve.tensor_scalar_add(xn[:, cu, :, TOKEN], xn[:, cu, :, TOKEN], 2.0 * NODES)
                        last = dve.tensor_tensor(tsum[:, 0, :], top[:, :, 0], top[:, :, 1], ALU.add)
                    if k == 6:
                        dve.tensor_tensor(
                            hot[:, :, :, :].rearrange("p t k e -> p (t k) e"),
                            m.small[:, 0:EXPERTS].unsqueeze(1).to_broadcast([P, TILES * TOP, EXPERTS]),
                            topf[:, :, :].rearrange("p t k -> p (t k)").unsqueeze(2).to_broadcast(
                                [P, TILES * TOP, EXPERTS]), ALU.is_equal)
                        last = dve.tensor_scalar_add(tsum[:, 0, :], tsum[:, 0, :], 1e-9)
                    if k == 7:
                        dve.tensor_tensor(given[:, :, :], hot[:, :, 0, :], hot[:, :, 1, :], ALU.add)
                        dve.tensor_copy(m.counts[:, 0, :], m.counts[:, TILES, :])
                        last = dve.reciprocal(tsum[:, 1, :], tsum[:, 0, :])
                    if k == 8:
                        dve.tensor_tensor(m.gates[:, bass.ds(c * TILES, TILES), :], top[:, :, 0:TOP],
                                          tsum[:, 1, :].unsqueeze(2).to_broadcast([P, TILES, TOP]),
                                          ALU.mult)
                    if k >= 8:
                        t = k - 8
                        last = dve.tensor_tensor(m.counts[:, t + 1, :], m.counts[:, t, :],
                                                 given[:, t, :], ALU.add)
                    last.then_inc(chosen, 1)

                def pick_rows(c, cu, k):
                    if k == 0:
                        dve.wait_ge(rank_psum, c + 1)
                        dve.tensor_tensor(rank[:, :, :], RANKS.rearrange("p (t e) -> p t e", e=EXPERTS),
                                          m.small[:, EXPERTS:2 * EXPERTS].unsqueeze(1).to_broadcast(
                                              [P, TILES, EXPERTS]), ALU.add).then_inc(rank_read, 1)
                    if k == 1:
                        dve.wait_ge(rank_read, c + 1)
                        dve.tensor_tensor(
                            picked[:, :, :, :], hot[:, :, :, :],
                            rank[:, :, :].unsqueeze(2).to_broadcast([P, TILES, TOP, EXPERTS]), ALU.mult
                            ).then_inc(picked_ready, 1)
                    if k == 2:
                        dve.wait_ge(picked_ready, c + 1)
                        dve.tensor_reduce(posf[:, :, :], picked[:, :, :, :], AX.X, ALU.add
                                          ).then_inc(posf_ready, 1)
                    if k == 3:
                        dve.wait_ge(posf_ready, c + 1)
                        dve.tensor_copy(pos2[:, cu, :, :], posf[:, :, :]).then_inc(pos_ready, 1)

                def body(b, n, u, scores, maxima, tail, route, rows):
                    for s in range(SLOTS):
                        for half in (0, 1):
                            if half == 0 and maxima:
                                i = SLOTS * (b + 1) + s
                                g, col = s // HALF, (s % HALF // 2) * TILES + 2 * (s % 2)
                                dve.wait_ge(sm_ready, i + 1)
                                dve.tensor_reduce(mx[:, 2 * (1 - u) + g, col:col + 2], SM[s % 2], AX.X,
                                                  ALU.max, negate=True).then_inc(max_done, 1)
                            if half == 1 and scores and s not in POOL_SLOTS:
                                if s == min(set(range(SLOTS)) - set(POOL_SLOTS)):
                                    dve.wait_ge(adj_ready, b + 1)
                                dve.wait_ge(exp_ready, EXPS * b + 2 * s + 2)
                                dve.tensor_tensor(ex[:, s % RING, :, :], ex[:, s % RING, :, :],
                                                  adj[:, u, s % HALF // 2, :].unsqueeze(1).to_broadcast(
                                                      [P, 2, NODES]), ALU.mult).then_inc(made_dve, 1)
                            if route and s == 0:
                                shift_logits(b - 2, half)
                            if scores and 2 <= s < 4 and 2 * (s - 2) + half < 3:
                                low_parts(b, 1, 2 * (s - 2) + half)
                            if route and (s, half) in CHOICE_AT:
                                choose(b - 2, u, CHOICE_AT.index((s, half)))
                            if tail and s == 4:
                                normalise(b - 1, 1, half)
                            if tail and (s, half) in STATS_AT:
                                norm_stats(b - 1, STATS_AT.index((s, half)))
                            if maxima and s in (10, 11) and 2 * (s - 10) + half < 3:
                                low_parts(b + 1, 0, 2 * (s - 10) + half)
                            if route and (s, half) in PICK_AT:
                                pick_rows(b - 2, u, PICK_AT.index((s, half)))
                            if scores and s == 12:
                                normalise(b, 0, half)
                            if tail and s == 12 and half == 0:
                                norm_shift(b - 1)
                every_window(body)(dve)
                dve.wait_ge(pos_ready, GRAPHS)
                tables.vector(dve)

            @block.tensor
            def _(pe):
                def body(b, n, u, scores, maxima, tail, route, rows):
                    v, nv = 1 - u, n + u

                    def values(vb, vu, s):
                        t, g = s % HALF // 2, s // HALF
                        if t == 0:
                            wait_pos(pe, osb_ready, 2 * vb + g)
                            if g == 0:
                                pe.wait_ge(v_placed, vb + 1)
                        pe.wait_ge(made_dve, N_DVE * vb + dve_made(s + 1))
                        wait_pos(pe, made_pool, N_POOL * vb + pool_made(s + 1))
                        for j in range(GROUP):
                            last = pe.matmul(OT[32 * j:32 * j + 32, :],
                                             vp[:, vu, t, g * GROUP + j, :],
                                             ex[:, (s + j // 2) % RING, j % 2, :],
                                             start=(t == 0), stop=(t == TILES - 1),
                                             skip_group_check=True)
                        last.then_inc(pv_done, 1)

                    def turn_max(bb, g, buf):
                        pe.wait_ge(max_done, SLOTS * bb + HALF * g + HALF)
                        pe.transpose(MISC[0:16, 0:P], mx[:, buf, :], m.ident[:, :]).then_inc(mt_psum, 1)

                    def turn_values(bb, g):
                        pe.wait_ge(osb_ready, 2 * bb + g + 1)
                        for t in range(TILES):
                            last = pe.transpose(MISC[:, t * P:(t + 1) * P], osb[:, t * P:(t + 1) * P],
                                                m.ident[:, :])
                        last.then_inc(ot_psum, 1)

                    for s in range(SLOTS):
                        if scores:
                            kt, pair, g = s % HALF // 2, s % 2, s // HALF
                            buf = 2 * u + g
                            if s % HALF == 0:
                                pe.wait_ge(shift_loaded[buf], 48 * n + 48)
                            for h in (0, 1):
                                wait_pos(pe, exp_ready, EXPS * b + 2 * s + h - 1)
                                pe.matmul(ST[h], ks[0:ROWS + 3, buf, 2 * pair + h, kt * P:(kt + 1) * P],
                                          qs[0:ROWS + 3, buf, 2 * pair + h, :], start=True, stop=True
                                          ).then_inc(st_ready, 1)
                        if maxima:
                            g = s // HALF
                            buf = 2 * v + g
                            hl, q0 = s % HALF // 2, 2 * (s % 2)
                            if s % HALF == 0:
                                pe.wait_ge(qk_loaded[buf], QK_DMAS * nv + QK_DMAS)
                            wait_pos(pe, max_done, SLOTS * (b + 1) + s - 1)
                            for q in (0, 1):
                                last = pe.matmul(SM[s % 2][:, q, :],
                                                 qs[0:ROWS, buf, hl, (q0 + q) * P:(q0 + q + 1) * P],
                                                 ks[0:ROWS, buf, hl, :], start=True, stop=True)
                            last.then_inc(sm_ready, 1)
                        if s % 2 == 0:
                            if s >= LAG and scores:
                                values(b, u, s - LAG)
                            if s < LAG and tail:
                                values(b - 1, 1 - u, SLOTS + s - LAG)

                        if s == 1 and route:
                            pe.wait_ge(xnT_ready, b - 1)
                            for t in range(TILES):
                                last = pe.matmul(MISC[:, t * EXPERTS:(t + 1) * EXPERTS],
                                                 xnT[:, t * P:(t + 1) * P], m.router[:, :],
                                                 start=True, stop=True)
                            last.then_inc(lg_psum, 1)
                        if s == 3 and scores:
                            pe.wait_ge(mt_rest, 2 * b + 1)
                            wait_pos(pe, an_ready, 2 * b - 1)
                            wait_pos(pe, lg_read, b - 1)
                            turn_max(b, 1, 2 * u + 1)
                        if s == 5 and tail:
                            if scores:
                                pe.wait_ge(mt_rest, 2 * b + 2)
                            elif route:
                                pe.wait_ge(lg_read, b - 1)
                            turn_values(b - 1, 1)
                        if s == 7 and tail:
                            pe.wait_ge(an_ready, 2 * b)
                            for t in range(TILES):
                                last = pe.transpose(MISC[:, t * P:(t + 1) * P], an[:, t, :], m.ident[:, :])
                            last.then_inc(at_psum, 1)
                        if s == 9 and tail:
                            pe.wait_ge(at_ready, b)
                            pe.matmul(MISC, m.ident[:, :],
                                      m.x[:, bass.ds((b - 1) * TILES, TILES), :].rearrange(
                                          "p t c -> p (t c)"), start=True, stop=False)
                            for t in range(TILES):
                                last = pe.matmul(MISC[:, t * P:(t + 1) * P], anT[:, t * P:(t + 1) * P],
                                                 m.wo[:, :], start=False, stop=(t == TILES - 1))
                            last.then_inc(wo_psum, 1)
                        if s == 11 and tail:
                            wait_pos(pe, x1_ready, b)
                        if s == 11 and route:
                            pe.wait_ge(chosen, CHOICE * (b - 1))
                            pe.matmul(RANKS, m.before[:, :], given[:, :, :].rearrange("p t e -> p (t e)"),
                                      start=True, stop=False)
                            pe.matmul(RANKS, m.ones[:, :],
                                      m.counts[:, 0:TILES, :].rearrange("p t e -> p (t e)"),
                                      start=False, stop=True).then_inc(rank_psum, 1)
                        if s == 11 and maxima:
                            turn_max(b + 1, 0, 2 * v)
                        if s == 13 and scores:
                            if maxima:
                                pe.wait_ge(mt_rest, 2 * b + 3)
                            if route:
                                pe.wait_ge(rank_read, b - 1)
                            turn_values(b, 0)
                        if s == 15 and tail:
                            if scores:
                                pe.wait_ge(an_ready, 2 * b + 1)
                            elif route:
                                pe.wait_ge(rank_read, b - 1)
                            pe.wait_ge(xn_ready, b)
                            for t in range(TILES):
                                last = pe.transpose(MISC[:, t * P:(t + 1) * P], xn[:, 1 - u, t, 0:HID],
                                                    m.ident[:, :])
                            last.then_inc(xnT_psum, 1)
                every_window(body)(pe)
                pe.wait_ge(chosen, CHOICE * GRAPHS)
                tables.tensor(pe)


def stage_experts(nc, m, w13_d, w2_d, rows_d, outs_d):
    with ExitStack() as ctx:
        def sb(name, shape, dt=F32):
            return ctx.enter_context(nc.sbuf_tensor(name, shape, dt))

        def sem(name):
            return ctx.enter_context(nc.semaphore(name))

        NB = N_BLOCKS
        xT = sb("block_T", [P, 2, BLOCK])
        xT_parts = sb("block_T_parts", [P, 2, 2, BLOCK], F32R)
        w13_parts = sb("w13_parts", [P, 2, 2, 2 * FT * P], F32R)
        xr, w13, w2 = m.xr, m.w13, m.w2
        rows_loaded = [sem(f"block_rows_loaded{q}") for q in range(DEEP)]
        act1 = sb("silu_h1", [P, 2, FT, BLOCK])
        hid = sb("hidden", [P, 2, FT, BLOCK])
        yr = sb("block_out", [P, DEEP, SUB, HID])
        second = sb("offset_if_second", [P, DEEP, SUB])
        odd_empty = sb("offset_if_empty", [P, DEEP, SUB])
        token_ready = sem("token_added")
        dest = sb("row_of_result", [P, DEEP, SUB], mybir.dt.uint32)

        xT_psum, xT_ready, h_psum, act_ready, hid_ready, y_psum, y_ready = (sem(n) for n in (
            "block_turned", "block_T_ready", "h_ready", "silu_ready", "hidden_ready", "y_summed", "y_ready"))
        w_high, x_high, x_split = (sem(n) for n in (
            "weights_high", "rows_high", "rows_split"))
        off_ready, dest_ready = sem("offset_ready"), sem("dest_ready")
        y_out = [sem(f"block_stored{q}") for q in range(DEEP)]

        H = [m.psum[:, 0:FT, :], m.psum[:, FT:2 * FT, :]]
        XT, Y = m.psum[:, 6, :], m.psum[:, 7, :]

        def every_block(step):
            def walk(eng):
                with eng.Fori(0, NB // DEEP) as i:
                    for q in range(DEEP):
                        step(DEEP * i + q, i, q)
            return walk

        def staggered(step):
            def walk(eng):
                step(0, 0, 0)
                with eng.Fori(0, NB // DEEP - 1) as i:
                    for c in range(1, DEEP + 1):
                        step(DEEP * i + c, i + c // DEEP, c % DEEP)
                for j in range(NB - DEEP + 1, NB + 1):
                    step(j, j // DEEP, j % DEEP)
            return walk

        def is_int(j, *values):
            return isinstance(j, int) and j in values

        with nc.Block() as block:
            @block.gpsimd
            def _(pool):
                def step(j, r, q):
                    if q >= 2:
                        wait_alone(pool, m, y_out[q - 2], 16 * SUB * (r + 1))
                    else:
                        wait_alone(pool, m, y_out[q + 2], 16 * SUB * r)
                    wait_alone(pool, m, y_ready, j + 1 + 1)
                    wait_alone(pool, m, dest_ready, j + 1)
                    for t in range(SUB):
                        pool.indirect_dma_start(
                            outs_d[:, :], bass.IndirectOffsetOnAxis(ap=dest[:, q, t:t + 1], axis=0),
                            yr[:, q, t, :], None).then_inc(y_out[q], 16)
                every_block(step)(pool)
                for q in range(DEEP):
                    pool.wait_ge(y_out[q], 16 * SUB * (NB // DEEP))

            @block.vector
            def _(dve):
                dve.sem_inc(hid_ready, 2)
                dve.sem_inc(act_ready, 2)

                def split_weights(j, r, q):
                    dve.wait_ge(m.w13_loaded[q], 16 * r + 16)
                    wait_pos(dve, h_psum, j - 1)
                    high, low = w13_parts[:, q % 2, 0, :], w13_parts[:, q % 2, 1, :]
                    whole = w13[:, q, :, :, :].rearrange("p a t h -> p (a t h)")
                    dve.tensor_copy(high, whole).then_inc(w_high, 1)
                    dve.wait_ge(w_high, j + 1)
                    dve.tensor_tensor(low, whole, high.bitcast(F32), ALU.subtract)

                def split_rows(j, q):
                    dve.wait_ge(xT_ready, j + 1)
                    high, low = xT_parts[:, q % 2, 0, :], xT_parts[:, q % 2, 1, :]
                    dve.tensor_copy(high, xT[:, q % 2, :]).then_inc(x_high, 1)
                    dve.wait_ge(x_high, j + 1)
                    dve.tensor_tensor(low, xT[:, q % 2, :], high.bitcast(F32), ALU.subtract
                                      ).then_inc(x_split, 1)

                def step(j, r, q):
                    if is_int(j, NB):
                        return
                    nxt = (j + 1, r + (q + 1) // DEEP, (q + 1) % DEEP)
                    if not is_int(j, NB - 1):
                        split_weights(*nxt)
                        split_rows(nxt[0], nxt[2])
                    wait_pos(dve, y_out[q], 16 * SUB * r)
                    dve.wait_ge(rows_loaded[q], 16 * r + 16)
                    dve.tensor_scalar(second[:, q, :], xr[:, q, :, FIRST], m.number[:, bass.ds(j, 1)],
                                      float(TOKENS), ALU.not_equal, ALU.mult).then_inc(off_ready, 1)
                    dve.wait_ge(off_ready, j + 1)
                    if q % 2:
                        dve.tensor_scalar(odd_empty[:, q, :], xr[:, q, :, FIRST], 0.0, float(BLOCK),
                                          ALU.is_lt, ALU.mult)
                        dve.tensor_tensor(second[:, q, :], second[:, q, :], xr[:, q, :, TOKEN], ALU.add
                                          ).then_inc(token_ready, 1)
                        wait_pos(dve, token_ready, 2 * r + q // 2 + 1)
                        dve.tensor_tensor(dest[:, q, :], second[:, q, :], odd_empty[:, q, :],
                                          ALU.add).then_inc(dest_ready, 1)
                    else:
                        dve.tensor_tensor(dest[:, q, :], second[:, q, :], xr[:, q, :, TOKEN],
                                          ALU.add).then_inc(dest_ready, 1)
                    dve.wait_ge(act_ready, j + 1 + 2)
                    wait_pos(dve, y_psum, j - 1)
                    dve.tensor_tensor(hid[:, q % 2, :, :], act1[:, q % 2, :, :],
                                      H[q % 2][:, :, BLOCK:2 * BLOCK], ALU.mult).then_inc(hid_ready, 1)
                split_weights(0, 0, 0)
                split_rows(0, 0)
                staggered(step)(dve)

            @block.sync
            def _(sp):
                def rows_in(j, q):
                    row = sp.value_load(m.src_i[0:1, bass.ds(j, 1)], min_val=0, max_val=TRASH)
                    sp.dma_start(xr[:, q, :, :], rows_d[bass.ds(row, BLOCK), :].rearrange(
                        "(p s) c -> p s c", s=SUB)).then_inc(rows_loaded[q], 16)

                for q in range(DEEP):
                    rows_in(q, q)
                    e = expert(sp, m, q)
                    if q >= EARLY:
                        w13_in(sp, m, w13_d, e, q)
                    w2_in(sp, m, w2_d, e, q)
                with sp.Fori(1, NB // DEEP) as i:
                    for q in range(DEEP):
                        j = DEEP * i + q
                        wait_alone(sp, m, h_psum, j - DEEP + 1)
                        wait_alone(sp, m, dest_ready, j - DEEP + 1)
                        e = expert(sp, m, j)
                        w13_in(sp, m, w13_d, e, q)
                        rows_in(j, q)
                        sp.wait_ge(y_psum, j - DEEP + 1)
                        w2_in(sp, m, w2_d, e, q)

            @block.tensor
            def _(pe):
                def turn(j, r, q):
                    pe.wait_ge(rows_loaded[q], 16 * r + 16)
                    for t in range(SUB):
                        last = pe.transpose(XT[:, t * P:(t + 1) * P], xr[:, q, t, 0:HID], m.ident[:, :])
                    last.then_inc(xT_psum, 1)

                def step(j, r, q):
                    if not is_int(j, NB):
                        pe.wait_ge(x_split, j + 1)
                        for t in range(FT):
                            for a in (0, 1):
                                c = (a * FT + t) * P
                                for i, (w, x) in enumerate(((0, 0), (0, 1), (1, 0))):
                                    last = pe.matmul(H[q % 2][:, t, a * BLOCK:(a + 1) * BLOCK],
                                                     w13_parts[:, q % 2, w, c:c + P],
                                                     xT_parts[:, q % 2, x, :],
                                                     start=(i == 0), stop=(i == 2))
                        last.then_inc(h_psum, 1)
                    if not is_int(j, NB - 1, NB):
                        turn(j + 1, r + (q + 1) // DEEP, (q + 1) % DEEP)
                    if not is_int(j, 0):
                        pe.wait_ge(hid_ready, j + 2)
                        pe.wait_ge(y_ready, j)
                        pe.wait_ge(m.w2_loaded[(q - 1) % DEEP], 16 * (r if q else r - 1) + 16)
                        for t2 in range(SUB):
                            for t in range(FT):
                                last = pe.matmul(Y[:, t2 * P:(t2 + 1) * P],
                                                 hid[:, (q - 1) % 2, t, t2 * P:(t2 + 1) * P],
                                                 w2[:, (q - 1) % DEEP, t, :],
                                                 start=(t == 0), stop=(t == FT - 1))
                        last.then_inc(y_psum, 1)
                turn(0, 0, 0)
                staggered(step)(pe)

            @block.scalar
            def _(act):
                act.sem_inc(y_ready, 1)

                def turned(j, q):
                    act.wait_ge(xT_psum, j + 1)
                    wait_pos(act, x_split, j - 1)
                    act.copy(xT[:, q % 2, :], XT[:, 0:BLOCK]).then_inc(xT_ready, 1)

                def step(j, r, q):
                    if not is_int(j, NB - 1, NB):
                        turned(j + 1, q + 1)
                    if not is_int(j, NB):
                        act.wait_ge(h_psum, j + 1)
                        act.wait_ge(hid_ready, j + 1)
                        act.activation(act1[:, q % 2, :, :], H[q % 2][:, :, 0:BLOCK], ACT.Silu
                                       ).then_inc(act_ready, 1)
                    if not is_int(j, 0):
                        act.wait_ge(y_psum, j)
                        wait_pos(act, y_out[(q - 1) % DEEP], 16 * SUB * (r if q else r - 1))
                        act.copy(yr[:, (q - 1) % DEEP, :, :],
                                 Y[:, 0:SUB * HID].rearrange("p (s c) -> p s c", s=SUB)
                                 ).then_inc(y_ready, 1)
                turned(0, 0)
                staggered(step)(act)


def stage_combine(nc, m, outs_d, out_d):
    with ExitStack() as ctx:
        def sb(name, shape, dt=F32):
            return ctx.enter_context(nc.sbuf_tensor(name, shape, dt))

        def sem(name):
            return ctx.enter_context(nc.semaphore(name))

        got = sb("results_of_choices", [P, DEEP, TOP, TILES, HID])
        res = sb("result", [P, DEEP, TILES, HID])
        loaded = [sem(f"results_loaded{q}") for q in range(DEEP)]
        stored = [sem(f"stored{q}") for q in range(DEEP)]
        gated, added, res_ready = sem("first_gated"), sem("choices_added"), sem("result_ready")

        def every_graph(step):
            def walk(eng):
                with eng.Fori(0, GRAPHS // DEEP) as i:
                    for q in range(DEEP):
                        step(DEEP * i + q, i, q)
            return walk

        with nc.Block() as block:
            @block.sync
            def _(sp):
                def load(b, q):
                    for k in range(TOP):
                        sp.dma_start(got[:, q, k, :, :],
                                     outs_d[bass.ds(b * NODES + k * TOKENS, NODES), :].rearrange(
                                         "(t p) c -> p t c", p=P)).then_inc(loaded[q], 16)

                def store(b, q):
                    sp.wait_ge(res_ready, b + 1)
                    sp.dma_start(out_d[b, :, :].rearrange("(t p) c -> p t c", p=P), res[:, q, :, :]
                                 ).then_inc(stored[q], 16)

                for q in range(DEEP):
                    load(q, q)
                with sp.Fori(0, GRAPHS // DEEP - 1) as i:
                    for q in range(DEEP):
                        b = DEEP * i + q
                        store(b, q)
                        load(b + DEEP, q)
                for q in range(DEEP):
                    store(GRAPHS - DEEP + q, q)
                for q in range(DEEP):
                    sp.wait_ge(stored[q], 16 * (GRAPHS // DEEP))

            @block.scalar
            def _(act):
                def step(b, r, q):
                    for t in range(TILES):
                        if t == 0:
                            wait_alone(act, m, loaded[q], 32 * r + 32)
                        last = act.activation(got[:, q, 0, t, :], got[:, q, 0, t, :], ACT.Copy,
                                              scale=m.gates[:, bass.ds(b * TILES + t, 1), 0])
                    last.then_inc(gated, 1)
                every_graph(step)(act)

            @block.vector
            def _(dve):
                def step(b, r, q):
                    dve.wait_ge(gated, b + 1)
                    for t in range(TILES):
                        last = dve.scalar_tensor_tensor(got[:, q, 1, t, :], got[:, q, 1, t, :],
                                                        m.gates[:, b * TILES + t, 1:2],
                                                        got[:, q, 0, t, :], ALU.mult, ALU.add)
                    last.then_inc(added, 1)
                every_graph(step)(dve)

            @block.gpsimd
            def _(pool):
                def step(b, r, q):
                    pool.wait_ge(added, b + 1)
                    wait_alone(pool, m, stored[q], 16 * r)
                    pool.tensor_tensor(res[:, q, :, :], got[:, q, 1, :, :],
                                       m.x[:, bass.ds(b * TILES, TILES), :], ALU.add
                                       ).then_inc(res_ready, 1)
                every_graph(step)(pool)


def build(nc, x, adjT, wq, wk, wv, wo, bo, router, before, small, blocks, w13, w2, out):
    with ExitStack() as ctx:
        m = place(nc, ctx)
        qk = nc.dram_tensor("qk_parts_dram", [GRAPHS, 6, P, NODES], BF16).ap()
        rows = nc.dram_tensor("rows_by_expert", [TRASH + BLOCK, WIDE], F32).ap()
        outs = nc.dram_tensor("outs_by_choice", [TOP * TOKENS + 2 * BLOCK, HID], F32).ap()
        stage_projections(nc, m, x, (wq, wk, wv, wo, bo, router, before, small, blocks), qk, adjT)
        stage_attention(nc, m, adjT, qk, rows, w13, w2)
        stage_experts(nc, m, w13, w2, rows, outs)
        stage_combine(nc, m, outs, out)


def layout(x, adj, Wq, Wk, Wv, Wo, bo, router_w, w1, w2, w3):
    import numpy as np

    c = np.ascontiguousarray
    by_place = np.arange(HID).reshape(HEADS, DH).T.reshape(-1)
    w13 = np.zeros((EXPERTS, HID, 2, FT * P), np.float32)
    w13[:, :, 0, :FFN] = w1.transpose(0, 2, 1)
    w13[:, :, 1, :FFN] = w3.transpose(0, 2, 1)
    w2p = np.zeros((EXPERTS, FT * P, HID), np.float32)
    w2p[:, :FFN, :] = w2.transpose(0, 2, 1)
    small = np.zeros((P, 2 * EXPERTS + TILES), np.float32)
    small[:, :EXPERTS] = np.arange(EXPERTS)
    small[:, EXPERTS:2 * EXPERTS] = np.arange(EXPERTS) * REGION
    small[:, 2 * EXPERTS:] = np.arange(NODES).reshape(TILES, P).T
    return {
        "x": c(x), "adjT": c(adj.transpose(0, 2, 1)),
        "wq": c(Wq[by_place].T), "wk": c(Wk[by_place].T), "wv": c(Wv.T), "wo": c(Wo.T),
        "bo": c(np.broadcast_to(bo, (P, HID))), "router": c(router_w.T),
        "before": np.triu(np.ones((P, P), np.float32), 1),
        "small": small,
        "blocks": c(np.broadcast_to(np.arange(N_BLOCKS, dtype=np.float32), (P, N_BLOCKS))),
        "w13": w13.reshape(EXPERTS, HID, 2 * FT * P),
        "w2": c(w2p.reshape(EXPERTS, FT, P, HID).transpose(0, 2, 1, 3)).reshape(EXPERTS, P, FT * HID),
    }


def kernel(x, adj, L0_gnn_Wq, L0_gnn_Wk, L0_gnn_Wv, L0_gnn_Wo, L0_gnn_bo, L0_ffn_router_w,
           L0_ffn_w1, L0_ffn_w2, L0_ffn_w3):
    import numpy as np
    import concourse.bacc as bacc
    from concourse.bass_utils import run_bass_kernel_spmd

    given = (x, adj, L0_gnn_Wq, L0_gnn_Wk, L0_gnn_Wv, L0_gnn_Wo, L0_gnn_bo, L0_ffn_router_w,
             L0_ffn_w1, L0_ffn_w2, L0_ffn_w3)
    arrays = layout(*(np.asarray(a) for a in given))
    nc = bacc.Bacc("TRN2", target_bir_lowering=False, num_devices=1)
    args = {k: nc.dram_tensor(k, a.shape, mybir.dt.from_np(a.dtype), kind="ExternalInput").ap()
            for k, a in arrays.items()}
    out = nc.dram_tensor("out", (GRAPHS, NODES, HID), F32, kind="ExternalOutput").ap()
    build(nc, **args, out=out)
    r = run_bass_kernel_spmd(nc, [arrays], core_ids=[0])
    return r.results[0]["out"]
```
